# Optimizing a Trainium2 kernel written in Bass

```python
import numpy as np
import jax
import jax.numpy as jnp

def _softmax(x, axis=-1):
    return jax.nn.softmax(x, axis=axis)

def _gelu(x):
    return jax.nn.gelu(x, approximate=True)

def _silu(x):
    return jax.nn.silu(x)

def _sigmoid(x):
    return jax.nn.sigmoid(x)

def _layernorm(x, axis=-1, eps=1e-05):
    m = jnp.mean(x, axis=axis, keepdims=True)
    v = jnp.var(x, axis=axis, keepdims=True)
    return (x - m) / jnp.sqrt(v + eps)

def _scatter_add(tgt, idx, src, axis=0):
    return tgt.at[idx].add(src)

def _segment_sum(src, seg, n):
    return jax.ops.segment_sum(src, seg, n)
kernel_name = 'mk_conv_preact_d4_conv_nchw256_r4_dbd8c4'

def setup_inputs(seed: int=0):
    np.random.seed(seed)
    _w = jnp.asarray

    def _rec_inputs():
        import jax
        import jax.numpy as jnp
        _gk = jax.random.key(seed)
        x = -0.0002023 + 1 * jax.random.normal(jax.random.fold_in(_gk, 1), (8, 64, 56, 56), jnp.float32)
        return x
    x = _rec_inputs()

    def _L0_conv_setup():
        import jax, jax.numpy as jnp
        import numpy as np
        B, C, H, W = (8, 64, 56, 56)
        K = 3
        S = 1
        D = 1
        HEAD = 1
        MID = int(C * 0.2)
        GAIN = float(np.sqrt(2.0))

        def _ddf_mul(x, cf, sf):
            p = D * (K - 1) // 2
            xp = jnp.pad(x, ((0, 0), (0, 0), (p, p), (p, p)))
            Ho, Wo = (H // S, W // S)
            out = jnp.zeros((B, C, Ho, Wo), x.dtype)
            for u in range(K):
                for v in range(K):
                    patch = xp[:, :, u * D:u * D + S * Ho:S, v * D:v * D + S * Wo:S]
                    out = out + patch * cf[:, :, u, v][:, :, None, None] * sf[:, u * K + v][:, None]
            return out
        key = jax.random.key(seed)
        ks = jax.random.split(key, 6)
        sc = 0.05
        return {'x': jax.random.normal(ks[0], (B, C, H, W), jnp.float32), 'w1': jax.random.normal(ks[1], (MID, C), jnp.float32) * sc, 'b1': jnp.zeros((MID,), jnp.float32), 'w2': jax.random.normal(ks[2], (C * K * K, MID), jnp.float32) * sc, 'b2': jnp.zeros((C * K * K,), jnp.float32), 'ws': jax.random.normal(ks[3], (HEAD * K * K, C), jnp.float32) * sc, 'bs': jnp.zeros((HEAD * K * K,), jnp.float32), 'fn_std': jax.random.normal(ks[4], (C * K * K,), jnp.float32) * (GAIN / K)}
    _L0_conv_all = _L0_conv_setup()
    _L0_conv_in = {k: v for k, v in _L0_conv_all.items() if k in ('w1', 'b1', 'w2', 'b2', 'ws', 'bs', 'fn_std')}
    del _L0_conv_all

    def _L1_conv_setup():
        import jax, jax.numpy as jnp
        import numpy as np
        B, C, H, W = (16, 64, 16, 16)
        CR = 64 // 8
        key = jax.random.key(seed)
        ks = jax.random.split(key, 7)
        s = 1.0 / np.sqrt(C)
        return {'x': jax.random.normal(ks[0], (B, C, H, W), dtype=jnp.float32), 'Wq': jax.random.uniform(ks[1], (CR, C), jnp.float32, -s, s), 'bq': jax.random.uniform(ks[2], (CR,), jnp.float32, -s, s), 'Wk': jax.random.uniform(ks[3], (CR, C), jnp.float32, -s, s), 'bk': jax.random.uniform(ks[4], (CR,), jnp.float32, -s, s), 'Wv': jax.random.uniform(ks[5], (C, C), jnp.float32, -s, s), 'bv': jax.random.uniform(ks[6], (C,), jnp.float32, -s, s)}
    _L1_conv_all = _L1_conv_setup()
    _L1_conv_in = {k: v for k, v in _L1_conv_all.items() if k in ('Wq', 'bq', 'Wk', 'bk', 'Wv', 'bv')}
    del _L1_conv_all

    def _L2_conv_setup():
        import jax, jax.numpy as jnp
        import numpy as np
        THRESHOLD = 0.05
        STRIDE = (1, 1)
        PADDING = ((1, 1), (1, 1))

        def ternary_quantize(w, threshold=THRESHOLD):
            mask = (jnp.abs(w) > threshold).astype(w.dtype)
            return jnp.sign(w) * mask
        key = jax.random.key(seed)
        k1, k2 = jax.random.split(key)
        B, Cin, H, W = (32, 64, 56, 56)
        Cout, kH, kW = (64, 3, 3)
        fan_in = Cin * kH * kW
        std = np.sqrt(2.0 / fan_in) * 2.0
        x = jax.random.normal(k1, (B, Cin, H, W), dtype=jnp.float32)
        weight = jax.random.normal(k2, (Cout, Cin, kH, kW), dtype=jnp.float32) * std
        bias = jnp.zeros((Cout,), dtype=jnp.float32)
        return {'x': x, 'weight': weight, 'bias': bias}
    _L2_conv_all = _L2_conv_setup()
    _L2_conv_in = {k: v for k, v in _L2_conv_all.items() if k in ('weight', 'bias')}
    del _L2_conv_all

    def _L3_conv_setup():
        import jax, jax.numpy as jnp
        import numpy as np
        key = jax.random.key(seed)
        k1, k2, k3, k4 = jax.random.split(key, 4)
        b, din, h, w = (4, 64, 16, 16)
        dk, dv = (16, 64)
        x = jax.random.normal(k1, (b, din, h, w), dtype=jnp.float32)
        q_w = jax.random.normal(k2, (dk, din), dtype=jnp.float32) * din ** (-0.5)
        k_w = jax.random.normal(k3, (dk, din), dtype=jnp.float32) * din ** (-0.5)
        v_w = jax.random.normal(k4, (dv, din), dtype=jnp.float32) * din ** (-0.5)
        return {'x': x, 'q_w': q_w, 'k_w': k_w, 'v_w': v_w}
    _L3_conv_all = _L3_conv_setup()
    _L3_conv_in = {k: v for k, v in _L3_conv_all.items() if k in ('q_w', 'k_w', 'v_w')}
    del _L3_conv_all
    return {'x': x, 'L0_conv_w1': _L0_conv_in['w1'], 'L0_conv_b1': _L0_conv_in['b1'], 'L0_conv_w2': _L0_conv_in['w2'], 'L0_conv_b2': _L0_conv_in['b2'], 'L0_conv_ws': _L0_conv_in['ws'], 'L0_conv_bs': _L0_conv_in['bs'], 'L0_conv_fn_std': _L0_conv_in['fn_std'], 'L1_conv_Wq': _L1_conv_in['Wq'], 'L1_conv_bq': _L1_conv_in['bq'], 'L1_conv_Wk': _L1_conv_in['Wk'], 'L1_conv_bk': _L1_conv_in['bk'], 'L1_conv_Wv': _L1_conv_in['Wv'], 'L1_conv_bv': _L1_conv_in['bv'], 'L2_conv_weight': _L2_conv_in['weight'], 'L2_conv_bias': _L2_conv_in['bias'], 'L3_conv_q_w': _L3_conv_in['q_w'], 'L3_conv_k_w': _L3_conv_in['k_w'], 'L3_conv_v_w': _L3_conv_in['v_w']}

def reference(x, L0_conv_w1, L0_conv_b1, L0_conv_w2, L0_conv_b2, L0_conv_ws, L0_conv_bs, L0_conv_fn_std, L1_conv_Wq, L1_conv_bq, L1_conv_Wk, L1_conv_bk, L1_conv_Wv, L1_conv_bv, L2_conv_weight, L2_conv_bias, L3_conv_q_w, L3_conv_k_w, L3_conv_v_w):
    import jax
    import jax.numpy as jnp

    def _L0_conv_ref(x, w1, b1, w2, b2, ws, bs, fn_std):
        import jax, jax.numpy as jnp
        import numpy as np
        B, C, H, W = (8, 64, 56, 56)
        K = 3
        S = 1
        D = 1
        HEAD = 1
        MID = int(C * 0.2)
        GAIN = float(np.sqrt(2.0))

        def _ddf_mul(x, cf, sf):
            p = D * (K - 1) // 2
            xp = jnp.pad(x, ((0, 0), (0, 0), (p, p), (p, p)))
            Ho, Wo = (H // S, W // S)
            out = jnp.zeros((B, C, Ho, Wo), x.dtype)
            for u in range(K):
                for v in range(K):
                    patch = xp[:, :, u * D:u * D + S * Ho:S, v * D:v * D + S * Wo:S]
                    out = out + patch * cf[:, :, u, v][:, :, None, None] * sf[:, u * K + v][:, None]
            return out
        pooled = x.mean((2, 3))
        y = jax.nn.relu(pooled @ w1.T + b1)
        y = (y @ w2.T + b2).reshape(B, C, K * K)
        y = (y - y.mean(-1, keepdims=True)) / (y.std(-1, ddof=1, keepdims=True) + 1e-10)
        cf = (y.reshape(B, C * K * K) * fn_std).reshape(B, C, K, K)
        xs = x[:, :, ::S, ::S]
        sf = jnp.einsum('bchw,nc->bnhw', xs, ws) + bs[None, :, None, None]
        sf = sf.reshape(B, HEAD, K * K, H // S, W // S)
        sf = (sf - sf.mean(2, keepdims=True)) / (sf.std(2, ddof=1, keepdims=True) + 1e-10)
        sf = sf.reshape(B, HEAD * K * K, H // S, W // S) * (GAIN / K)
        return _ddf_mul(x, cf, sf)

    def _L1_conv_ref(x, Wq, bq, Wk, bk, Wv, bv):
        import jax, jax.numpy as jnp
        import numpy as np
        B, C, H, W = (16, 64, 16, 16)
        CR = 64 // 8
        q = jnp.einsum('bchw,oc->bohw', x, Wq) + bq[None, :, None, None]
        k = jnp.einsum('bchw,oc->bohw', x, Wk) + bk[None, :, None, None]
        v = jnp.einsum('bchw,oc->bohw', x, Wv) + bv[None, :, None, None]
        k_mean = jnp.mean(k, axis=(2, 3))
        att = jax.nn.sigmoid(jnp.einsum('bohw,bo->bhw', q, k_mean))[:, None]
        return v * att

    def _L2_conv_ref(x, weight, bias):
        import jax, jax.numpy as jnp
        import numpy as np
        THRESHOLD = 0.05
        STRIDE = (1, 1)
        PADDING = ((1, 1), (1, 1))

        def ternary_quantize(w, threshold=THRESHOLD):
            mask = (jnp.abs(w) > threshold).astype(w.dtype)
            return jnp.sign(w) * mask
        w_t = ternary_quantize(weight, THRESHOLD)
        out = jax.lax.conv_general_dilated(x, w_t, window_strides=STRIDE, padding=PADDING, dimension_numbers=('NCHW', 'OIHW', 'NCHW'))
        return out + bias[None, :, None, None]

    def _L3_conv_ref(x, q_w, k_w, v_w):
        import jax, jax.numpy as jnp
        import numpy as np
        b, din, h, w = x.shape
        hw = h * w
        xf = x.reshape(b, din, hw)
        Q = jnp.einsum('kc,bcp->bkp', q_w, xf)
        K = jnp.einsum('kc,bcp->bkp', k_w, xf)
        V = jnp.einsum('vc,bcp->bvp', v_w, xf)
        S = jnp.einsum('bkp,bkq->bpq', Q, K)
        A = jax.nn.softmax(S, axis=-1)
        z = jnp.einsum('bpq,bvq->bvp', A, V)
        return z.reshape(b, V.shape[1], h, w)

    def _gn(v, G=32, eps=1e-05):
        B_, C_, H_, W_ = v.shape
        g = v.reshape(B_, G, C_ // G, H_, W_)
        m = jnp.mean(g, axis=(2, 3, 4), keepdims=True)
        s = jnp.var(g, axis=(2, 3, 4), keepdims=True)
        return ((g - m) / jnp.sqrt(s + eps)).reshape(v.shape)

    def _ln_c(v, eps=1e-06):
        m = jnp.mean(v, axis=1, keepdims=True)
        s = jnp.var(v, axis=1, keepdims=True)
        return (v - m) / jnp.sqrt(s + eps)

    def _ln_t(v, eps=1e-05):
        m = jnp.mean(v, axis=-1, keepdims=True)
        s = jnp.var(v, axis=-1, keepdims=True)
        return (v - m) / jnp.sqrt(s + eps)

    def _to_tokens(v):
        B_, C_, H_, W_ = v.shape
        return v.reshape(B_, C_, H_ * W_).transpose(0, 2, 1)

    def _from_tokens(t, like):
        B_, C_, H_, W_ = like.shape
        return t.transpose(0, 2, 1).reshape(B_, C_, H_, W_)
    x = x + _L0_conv_ref(_gn(x), L0_conv_w1, L0_conv_b1, L0_conv_w2, L0_conv_b2, L0_conv_ws, L0_conv_bs, L0_conv_fn_std)
    x = x + _L1_conv_ref(_gn(x), L1_conv_Wq, L1_conv_bq, L1_conv_Wk, L1_conv_bk, L1_conv_Wv, L1_conv_bv)
    x = x + _L2_conv_ref(_gn(x), L2_conv_weight, L2_conv_bias)
    x = x + _L3_conv_ref(_gn(x), L3_conv_q_w, L3_conv_k_w, L3_conv_v_w)
    return x

_drawn_inputs = setup_inputs


def setup_inputs(seed=0):
    import zlib

    import numpy as np

    out = dict(_drawn_inputs(seed))
    spreads = {'L0_conv_b1': (0.0, 0.1),
     'L0_conv_b2': (0.0, 0.1),
     'L0_conv_bs': (0.0, 0.1),
     'L2_conv_bias': (0.0, 0.8)}
    factors = {'L0_conv_w1': 8.0,
     'L1_conv_Wq': 3.562,
     'L1_conv_bq': 28.826,
     'L1_conv_Wk': 8.0,
     'L1_conv_bk': 3.068}
    for name, (base, spread) in spreads.items():
        noise = np.random.default_rng([zlib.crc32(name.encode()), seed]).standard_normal(out[name].shape)
        drawn = base * np.exp(spread * noise) if base else spread * noise
        out[name] = jnp.asarray(drawn.astype(out[name].dtype))
    for name, factor in factors.items():
        out[name] = (out[name] * factor).astype(out[name].dtype)
    return out
```

```python
from contextlib import ExitStack

import concourse.bass as bass
from concourse import mybir

F32 = mybir.dt.float32
F32R = mybir.dt.float32r
BF16 = mybir.dt.bfloat16
ALU = mybir.AluOpType
ACT = mybir.ActivationFunctionType
X = mybir.AxisListType.X
ds = bass.ds

B, C, H, W = 8, 64, 56, 56
P = 2 * C
GROUPS = B // 2
HW = H * W
ROWS = 8
CH = ROWS * W
NJ = HW // CH
PW = W + 2
PADDED = PW * (H + 2) + 4
TAPS = 9
MID = 12
CR = 8
DK = 16
GAIN_OVER_K = float(2.0 ** 0.5) / 3
THRESHOLD = 0.05
SP2 = 2 * PW
NSP = H // 2
PART = 2 * TAPS
PITCH = 32
QC = 128
NQ = -(-HW // QC)
KROWS = 6 * DK
BLK = CH // 4
NMAX = 2 * 4 * NJ
PSLOTS = 5
TAP_BANKS = 3
POOL_TAPS = 4
DVE_SUMS = (3, 7, 11, 15, 19, 23, 24)
LAST_MAX_STEP = 20

COLS = {}
_at = 0
for _name, _n in (("w1", 2 * MID), ("ws", PART), ("wv", P), ("wk", 2 * CR), ("qk3", 4 * DK), ("wv3", P),
                  ("w2", TAPS * P), ("wq", P), ("conv", TAPS * P)):
    COLS[_name] = (_at, _at + _n)
    _at += _n
WCOLS = _at
VEC = {"b2": (0, 9), "fn": (9, 18), "b1": (18, 19), "bk": (19, 20), "bq": (20, 21), "bv": (21, 22),
       "bc": (22, 23), "bs": (23, 32)}
VCOLS = 32
CST = {"ident": (0, P), "pair": (P, 2 * P), "half": (2 * P, 3 * P), "half8": (3 * P, 4 * P),
       "sel": (4 * P, (4 + TAPS) * P)}
CCOLS = (4 + TAPS) * P


def key_rows(j):
    return min(QC, HW - j * QC)


def pool_sums_upto(j):
    return sum(1 for i in range(max(j, 1) + 1) if i not in DVE_SUMS)


def dve_sums_upto(j):
    return sum(1 for i in range(j + 1) if i in DVE_SUMS)


POOL_SUMS = pool_sums_upto(NQ - 1)
NDVE = len(DVE_SUMS)


def max_tiles_at(j):
    n = LAST_MAX_STEP + 1
    return range(NMAX * min(j, n) // n, NMAX * min(j + 1, n) // n)


def build(nc, x, w1t, b1, w2t, b2, wst, bs, fn, wq, bq, wkt, bk, wvt, bv, wc, bc, q3t, k3t, v3t, cst, out):
    with ExitStack() as ctx:
        def sb(name, shape, dt=F32):
            return ctx.enter_context(nc.sbuf_tensor(name, shape, dt))

        def sem(name):
            return ctx.enter_context(nc.semaphore(name))

        xin = sb("xin", [P, HW])
        xw = sb("xw", [P, HW])
        xnp = sb("xnp", [P, PADDED])
        xh = sb("xh", [P, PADDED], F32R)
        xl = sb("xl", [P, PADDED], F32R)
        xnf = sb("xnf", [P, HW])
        wz = sb("wz", [P, WCOLS])
        wt = sb("wt", [P, TAPS * P], F32R)
        vec = sb("vec", [P, VCOLS])
        cs = sb("cs", [P, CCOLS])
        selb = sb("selb", [3 * PITCH, TAPS, P], BF16)
        identb = sb("identb", [P, P], BF16)
        ones = sb("ones", [P, C])
        mhalf = sb("mhalf", [P, 64])
        phalf = sb("phalf", [P, 64])
        st6 = sb("st6", [P, NJ, 6])
        mv = sb("mv", [P, 2])
        idle = sb("idle", [P, 1])
        dm = sb("dm", [P, 1])
        sq = sb("sq", [P, 1])
        ve = sb("ve", [P, 1])
        rstd = sb("rstd", [P, 1])
        nb = sb("nb", [P, 1])
        pooled = sb("pooled", [P, 2])
        y1 = sb("y1", [2 * MID, 1])
        yf = sb("yf", [P, TAPS])
        ysq = sb("ysq", [P, TAPS])
        ys = sb("ys", [P, 6])
        cf = sb("cf", [P, TAPS])
        sf = sb("sf", [SP2, NSP * 2, TAPS])
        sf2 = sb("sf2", [SP2, NSP * 2, TAPS])
        sfs = sb("sfs", [SP2, 5, NSP * 2])
        sfp = sb("sfp", [SP2, NSP, 3, PITCH], BF16)
        km = sb("km", [2 * CR, 2])
        uc = sb("uc", [P, 2])
        U = sb("U", [P, P])
        parts = sb("parts", [4 * DK, 3, HW], BF16)
        rest = sb("rest", [4 * DK, 2, CH])
        Qa = sb("Qa", [P, 2, HW], BF16)
        Ka = sb("Ka", [P, 2, HW], BF16)
        VT = sb("VT", [QC, NQ, P])
        Pb = sb("Pb", [QC, PSLOTS, 2, CH])
        flat = Pb[:, :, :, :].rearrange("p a b c -> p (a b c)")
        tneg = flat[:, 0:TAPS * P]
        prod = flat[:, 0:TAPS * CH].rearrange("p (t n) -> p t n", t=TAPS)
        flat = VT[:, :, :].rearrange("p a b -> p (a b)")
        pu = flat[:, 0:3 * CH].rearrange("p (a n) -> p a n", a=3)
        SF = Qa[0:3 * PITCH, 0, :]
        accP = sb("accP", [QC, 2, CH])
        accD = sb("accD", [QC, 2, CH])
        att, gated = accP, accD
        nmt = sb("nmt", [BLK, NMAX])
        nm = sb("nm", [BLK, 2, 8])
        mp = sb("mp", [BLK, 8, 3], BF16)
        Osb = sb("Osb", [P, CH])
        Rr = sb("Rr", [P, CH])
        fin = sb("fin", [P, CH])

        PS = ctx.enter_context(nc.psum_tensor("PS", [P, 8, 512], F32))
        small = PS[:, 7, :]
        ACCB = 4
        MAXB = 4
        OB = 6
        sTb = PS[:, 0:NJ, :].bitcast(BF16)
        rowb = PS[:, 7, :].bitcast(BF16)

        def pad_rows(t, r0, n, c0=0):
            return t[:, r0 * PW + c0:(r0 + n) * PW + c0].rearrange("p (r w) -> p r w", w=PW)[:, :, 0:W]

        def pad_rows_at(t, off, n):
            return t[:, ds(off, n * PW)].rearrange("p (r w) -> p r w", w=PW)[:, :, 0:W]

        def rows(ap):
            return ap.rearrange("p (r w) -> p r w", w=W)

        def wcol(name):
            return wz[:, COLS[name][0]:COLS[name][1]]

        def v(name, n=P):
            return vec[0:n, VEC[name][0]:VEC[name][1]]

        identf = cs[:, CST["ident"][0]:CST["ident"][1]]
        pair = cs[:, CST["pair"][0]:CST["pair"][1]]
        halfm = cs[:, CST["half"][0]:CST["half"][1]]
        half8 = cs[:, CST["half8"][0]:CST["half8"][1]]

        zeroed = sem("weights_zeroed")
        w_loaded = sem("weights_loaded")
        borders = sem("borders_zeroed")
        consts = sem("constants_ready")
        x_loaded = sem("x_loaded")
        dve_step = sem("dve_step")
        gn_mean = [sem(f"gn_mean_{i}") for i in range(4)]
        gn_pm = [sem(f"gn_pair_mean_{i}") for i in range(4)]
        gn_sq = [sem(f"gn_squares_{i}") for i in range(4)]
        gn_pv = [sem(f"gn_pair_var_{i}") for i in range(4)]
        gn_ve = [sem(f"gn_var_eps_{i}") for i in range(4)]
        gn_rstd = [sem(f"gn_rstd_{i}") for i in range(4)]
        gn_nb = [sem(f"gn_bias_{i}") for i in range(4)]
        pooled_ready = sem("pooled_ready")
        xn_ready = [sem(f"xn_ready_{i}") for i in range(4)]
        mid_ready = sem("mid_ready")
        y1_ready = sem("y1_ready")
        y_ready = sem("y_ready")
        yvar_ready = sem("yvar_ready")
        ysd_ready = sem("ysd_ready")
        sfT_ready = sem("sfT_ready")
        sfvar_ready = sem("sfvar_ready")
        sfsd_ready = sem("sfsd_ready")
        sfp_ready = sem("sf_parts_ready")
        sft_ready = sem("sf_transposed")
        SF_ready = sem("SF_ready")
        tap_ready = sem("tap_ready")
        prod_ready = sem("prod_ready")
        accum_ready = sem("tap_sum_ready")
        pool_step = sem("pool_step")
        pooltaps = sem("pool_taps_summed")
        l0_done = sem("l0_chunk_done")
        km_ps = sem("km_in_psum")
        km_ready = sem("km_ready")
        u_ps = sem("u_in_psum")
        U_ready = sem("U_ready")
        l1_ps = sem("l1_in_psum")
        att_ready = sem("att_ready")
        gated_ready = sem("gated_ready")
        l1_done = sem("l1_chunk_done")
        xh_ready = sem("xh_ready")
        xl_ready = sem("xl_ready")
        conv_ready = sem("conv_ready")
        l2_done = sem("l2_chunk_done")
        qk_ps = sem("qk_in_psum")
        part_h = sem("qk_part_high")
        rest_h = sem("qk_rest")
        part_m = sem("qk_part_middle")
        part_l = sem("qk_part_low")
        qk_loaded = sem("qk_rows_loaded")
        v_ps = sem("v_in_psum")
        v_ready = sem("v_ready")
        mx_ready = sem("max_scores_ready")
        mx_free = sem("max_bank_free")
        mxstep = sem("max_split_step")
        negm = sem("negmax_parts_ready")
        mrow_ps = sem("max_rows_in_psum")
        mrow = sem("max_rows_ready")
        st_ready = sem("scores_ready")
        exp_done = sem("exp_done")
        pv_done = sem("pv_done")
        psum_pool = sem("exps_summed_by_pool")
        psum_dve = sem("exps_summed_by_dve")
        ocopy = sem("output_copied")
        d_ready = sem("denominators_ready")
        recip = sem("reciprocals_ready")
        fin_step = sem("normalised")
        fin_done = sem("l3_chunk_done")
        stored = sem("stored")

        loads = []
        for h in range(2):
            cc = slice(C * h, C * h + C)

            def blk(name, a, n, p=cc):
                return wz[p, COLS[name][0] + a:COLS[name][0] + a + n]
            loads += [
                (blk("w1", MID * h, MID), w1t), (blk("ws", TAPS * h, TAPS), wst), (blk("wv", C * h, C), wvt),
                (blk("wk", CR * h, CR), wkt), (blk("qk3", 2 * DK * h, DK), q3t),
                (blk("qk3", 2 * DK * h + DK, DK), k3t), (blk("wv3", C * h, C), v3t),
                (blk("wq", C * h, C, slice(CR * h, CR * h + CR)), wq),
                (wz[MID * h:MID * h + MID, COLS["w2"][0]:COLS["w2"][1]]
                 .rearrange("m (t c) -> m t c", t=TAPS)[:, :, cc], w2t),
                (wcol("conv")[cc].rearrange("m (t c) -> m t c", t=TAPS)[:, :, cc], wc),
                (v("b2")[cc], b2), (v("fn")[cc], fn), (v("bv")[cc], bv), (v("bc")[cc], bc),
                (vec[MID * h:MID * h + MID, 18:19], b1), (vec[CR * h:CR * h + CR, 19:20], bk),
                (vec[CR * h:CR * h + CR, 20:21], bq),
            ]
        loads += [(cs[:, :], cst), (v("bs"), bs.partition_broadcast(P))]
        LOADED = 16 * len(loads)
        LINKS = 31

        block = ctx.enter_context(nc.Block())

        @block.sync
        def _(sp):
            sp.dma_start(xin[:, :], x[0]).then_inc(x_loaded, 16)
            sp.sem_inc(stored, 16)
            sp.sem_inc(qk_loaded, 16)
            for first in (ocopy, d_ready, recip, fin_done):
                sp.sem_inc(first, 1)
            sp.wait_ge(zeroed, 1)
            for dst, src in loads:
                sp.dma_start(dst, src).then_inc(w_loaded, 16)

            def spread():
                for h in range(2):
                    for dst, base, order in ((Qa, 2 * DK * h, (0, 0, 1, 0, 2, 1)),
                                             (Ka, 2 * DK * h + DK, (0, 1, 0, 2, 0, 1))):
                        for r, part in enumerate(order):
                            sp.dma_start(dst[DK * r:DK * r + DK, h, :],
                                         parts[base:base + DK, part, :]).then_inc(qk_loaded, 16)

            def store(g):
                with sp.Fori(0, NJ) as s:
                    sp.wait_ge(fin_done, NJ * g + s + 2)
                    sp.dma_start(out[g][:, ds(s * CH, CH)], xw[:, ds(s * CH, CH)]).then_inc(stored, 16)

            def group(g, last):
                sp.wait_ge(part_l, NJ * g + NJ)
                spread()
                if not last:
                    sp.dma_start(xin[:, :], x[g + 1]).then_inc(x_loaded, 16)
                store(g)

            with sp.Fori(0, GROUPS - 1) as g:
                group(g, False)
            group(GROUPS - 1, True)
            sp.wait_ge(stored, 16 * (NJ * GROUPS + 1))

        def low_part(dve, g, j):
            c = slice(j * CH, (j + 1) * CH)
            dve.wait_ge(part_m, NJ * g + j + 1)
            nc.vector.tensor_tensor(parts[:, 2, c], rest[:, j % 2, :], parts[:, 1, c],
                                    ALU.subtract).then_inc(part_l, 1)

        @block.vector
        def _(dve):
            nc.vector.memset(wz[:, :], 0.0)
            nc.vector.memset(vec[:, :], 0.0).then_inc(zeroed, 1)
            nc.vector.memset(xnp[:, :], 0.0)
            nc.vector.memset(xh[:, :].bitcast(F32), 0.0)
            nc.vector.memset(xl[:, :].bitcast(F32), 0.0).then_inc(borders, 1)
            nc.vector.memset(ones[:, :], 1.0)
            nc.vector.memset(sfp[:, :, :, :], 0.0)
            nc.vector.memset(mhalf[:, :], -0.5)
            nc.vector.memset(VT[key_rows(NQ - 1):QC, NQ - 1, :], 0.0)
            nc.vector.memset(phalf[:, :], 0.5)
            nc.vector.memset(Ka[KROWS:KROWS + 3, :, :], 1.0)
            dve.sem_inc(prod_ready, TAP_BANKS)
            dve.sem_inc(mx_free, 2)
            dve.sem_inc(psum_dve, NDVE)
            dve.wait_ge(w_loaded, LOADED)
            nc.vector.tensor_copy(selb[:, :, :], cs[0:3 * PITCH, CST["sel"][0]:CST["sel"][1]]
                                  .rearrange("p (t c) -> p t c", t=TAPS))
            nc.vector.tensor_copy(identb[:, :], identf)
            nc.vector.tensor_scalar(tneg, wcol("conv"), -THRESHOLD, None, ALU.is_lt)
            nc.vector.tensor_scalar(wcol("conv"), wcol("conv"), THRESHOLD, None, ALU.is_gt).then_inc(consts, 1)
            dve.wait_ge(consts, 1)
            nc.vector.tensor_tensor(wt[:, :], wcol("conv"), tneg, ALU.subtract).then_inc(consts, 1)

            with dve.Fori(0, GROUPS) as g:
                n = [0]

                def link(ins):
                    n[0] += 1
                    ins.then_inc(dve_step, 1)
                    dve.wait_ge(dve_step, LINKS * g + n[0])

                def stats(layer, src):
                    for i in range(NJ):
                        last = nc.vector.bn_stats(st6[:, i, :], src[:, i * CH:(i + 1) * CH])
                    link(last)
                    nc.vector.memset(idle[:, :], 0.0)
                    nc.vector.bn_aggr(mv[:, :], st6[:, :, :].rearrange("p a b -> p (a b)")).then_inc(gn_mean[layer], 1)
                    dve.wait_ge(gn_pm[layer], g + 1)
                    link(nc.vector.tensor_tensor(dm[:, :], mv[:, 0:1], small[:, 0:1], ALU.subtract))
                    nc.vector.scalar_tensor_tensor(out=sq[:, :], in0=dm[:, :], scalar=dm[:, :], in1=mv[:, 1:2],
                                                   op0=ALU.mult, op1=ALU.add).then_inc(gn_sq[layer], 1)
                    dve.wait_ge(gn_pv[layer], g + 1)
                    nc.vector.tensor_scalar(ve[:, :], small[:, 1:2], 1e-5, None, ALU.add).then_inc(gn_ve[layer], 1)
                    dve.wait_ge(gn_rstd[layer], g + 1)
                    nc.vector.scalar_tensor_tensor(out=nb[:, :], in0=small[:, 0:1], scalar=-1.0, in1=rstd[:, :],
                                                   op0=ALU.mult, op1=ALU.mult).then_inc(gn_nb[layer], 1)

                dve.wait_ge(x_loaded, 16 * g + 16)
                stats(0, xin)
                nc.vector.tensor_tensor(pooled[:, 0:1], dm[:, :], rstd[:, :], ALU.mult).then_inc(pooled_ready, 1)
                dve.wait_ge(mid_ready, g + 1)
                nc.vector.tensor_scalar(y1[:, :], small[0:2 * MID, 2:3], v("b1", 2 * MID), 0.0,
                                        ALU.add, ALU.max).then_inc(y1_ready, 1)
                dve.wait_ge(y_ready, g + 1)
                link(nc.vector.tensor_tensor(yf[:, :], small[:, 8:8 + TAPS], v("b2"), ALU.add))
                link(nc.vector.reduce_sum(ys[:, 0:1], yf[:, :], X))
                link(nc.vector.tensor_scalar(ys[:, 1:2], ys[:, 0:1], 1.0 / TAPS, None, ALU.mult))
                link(nc.vector.tensor_scalar(yf[:, :], yf[:, :], ys[:, 1:2], None, ALU.subtract))
                link(nc.vector.tensor_tensor(ysq[:, :], yf[:, :], yf[:, :], ALU.mult))
                link(nc.vector.reduce_sum(ys[:, 2:3], ysq[:, :], X))
                nc.vector.tensor_scalar(ys[:, 3:4], ys[:, 2:3], 1.0 / (TAPS - 1), None, ALU.mult).then_inc(yvar_ready, 1)
                dve.wait_ge(ysd_ready, g + 1)
                link(nc.vector.tensor_scalar(ys[:, 5:6], ys[:, 4:5], 1e-10, None, ALU.add))
                link(nc.vector.reciprocal(ys[:, 0:1], ys[:, 5:6]))
                link(nc.vector.scalar_tensor_tensor(out=cf[:, :], in0=yf[:, :], scalar=ys[:, 0:1], in1=v("fn"),
                                                    op0=ALU.mult, op1=ALU.mult))

                def per_pixel(i):
                    return sfs[:, i, :].unsqueeze(2).to_broadcast([SP2, 2 * NSP, TAPS])

                dve.wait_ge(sfT_ready, g + 1)
                link(nc.vector.tensor_tensor(
                    sf[:, :, :], PS[0:SP2, OB, 0:2 * NSP * TAPS].rearrange("p (n t) -> p n t", t=TAPS),
                    v("bs", SP2).unsqueeze(1).to_broadcast([SP2, 2 * NSP, TAPS]), ALU.add))
                link(nc.vector.reduce_sum(sfs[:, 0, :], sf[:, :, :], X))
                link(nc.vector.tensor_scalar(sfs[:, 1, :], sfs[:, 0, :], 1.0 / TAPS, None, ALU.mult))
                link(nc.vector.tensor_tensor(sf[:, :, :], sf[:, :, :], per_pixel(1), ALU.subtract))
                link(nc.vector.tensor_tensor(sf2[:, :, :], sf[:, :, :], sf[:, :, :], ALU.mult))
                link(nc.vector.reduce_sum(sfs[:, 2, :], sf2[:, :, :], X))
                nc.vector.tensor_scalar(sfs[:, 3, :], sfs[:, 2, :], 1.0 / (TAPS - 1), None,
                                        ALU.mult).then_inc(sfvar_ready, 1)
                dve.wait_ge(sfsd_ready, g + 1)
                link(nc.vector.tensor_scalar(sfs[:, 0, :], sfs[:, 4, :], 1e-10, None, ALU.add))
                link(nc.vector.reciprocal(sfs[:, 2, :], sfs[:, 0, :]))
                link(nc.vector.scalar_tensor_tensor(out=sf[:, :, :], in0=sf[:, :, :], scalar=GAIN_OVER_K,
                                                    in1=per_pixel(2), op0=ALU.mult, op1=ALU.mult))
                sfv = sf[:, :, :].rearrange("p (n b) t -> p n (b t)", b=2)
                sf2v = sf2[:, :, :].rearrange("p (n b) t -> p n (b t)", b=2)
                link(nc.vector.tensor_copy(sfp[:, :, 0, 0:PART], sfv))
                link(nc.vector.tensor_tensor(sf2v, sfv, sfp[:, :, 0, 0:PART], ALU.subtract))
                link(nc.vector.tensor_copy(sfp[:, :, 1, 0:PART], sf2v))
                nc.vector.tensor_tensor(sfp[:, :, 2, 0:PART], sf2v, sfp[:, :, 1, 0:PART], ALU.subtract).then_inc(sfp_ready, 1)

                def tap(j, t):
                    k = NJ * g + j
                    dve.wait_ge(tap_ready, TAPS * k + t + 1)
                    if t < POOL_TAPS:
                        dve.wait_ge(pooltaps, k + 1)
                    else:
                        dve.wait_ge(accum_ready, k + 1)
                    nc.vector.scalar_tensor_tensor(
                        out=rows(prod[:, t, :]), in0=rows(PS[:, t % TAP_BANKS, 0:CH]), scalar=cf[:, t:t + 1],
                        in1=pad_rows_at(xnp, j * (ROWS * PW) + (t // 3) * PW + t % 3, ROWS),
                        op0=ALU.mult, op1=ALU.mult).then_inc(prod_ready, 1)

                def l0_sum(j):
                    dve.wait_ge(accum_ready, NJ * g + j + 2)
                    dve.wait_ge(pooltaps, NJ * g + j + 2)
                    nc.vector.tensor_tensor(xw[:, ds(j * CH, CH)], PS[:, ACCB, 0:CH], pu[:, 2, :],
                                            ALU.add).then_inc(l0_done, 1)

                dve.wait_ge(stored, 16 * (NJ * g + 1))
                for t in range(TAPS):
                    tap(0, t)
                with dve.Fori(1, NJ) as j:
                    for t in range(TAPS):
                        if t == POOL_TAPS:
                            l0_sum(j - 1)
                        tap(j, t)
                l0_sum(NJ - 1)

                dve.wait_ge(l0_done, NJ * g + NJ + 1)
                stats(1, xw)
                nc.vector.tensor_tensor(pooled[:, 1:2], dm[:, :], rstd[:, :], ALU.mult).then_inc(pooled_ready, 1)
                dve.wait_ge(km_ps, g + 1)
                link(nc.vector.tensor_tensor(km[:, 0:1], small[0:2 * CR, 20:21], v("bk", 2 * CR), ALU.add))
                nc.vector.tensor_tensor(km[:, 1:2], km[:, 0:1], v("bq", 2 * CR), ALU.mult).then_inc(km_ready, 1)
                dve.wait_ge(u_ps, g + 1)
                link(nc.vector.tensor_copy(uc[:, :], small[:, 21:23]))
                nc.vector.tensor_scalar(U[:, :], halfm, uc[:, 0:1], None, ALU.mult).then_inc(U_ready, 1)

                def l1_add(j):
                    dve.wait_ge(gated_ready, NJ * g + j + 1)
                    nc.vector.tensor_tensor(xw[:, j * CH:(j + 1) * CH], xw[:, j * CH:(j + 1) * CH],
                                            gated[:, j % 2, :], ALU.add).then_inc(l1_done, 1)

                for j in range(NJ):
                    dve.wait_ge(att_ready, NJ * g + j + 1)
                    if j >= 2:
                        dve.wait_ge(l1_done, NJ * g + j - 1)
                    nc.vector.scalar_tensor_tensor(out=gated[:, j % 2, :], in0=PS[:, j % 3, 0:CH], scalar=v("bv"),
                                                   in1=att[:, j % 2, :], op0=ALU.add,
                                                   op1=ALU.mult).then_inc(gated_ready, 1)
                    if j:
                        l1_add(j - 1)
                l1_add(NJ - 1)

                dve.wait_ge(l1_done, NJ * g + NJ)
                stats(2, xw)
                for j in range(NJ):
                    dve.wait_ge(xn_ready[2], NJ * g + j + 1)
                    nc.vector.tensor_tensor(pad_rows(xl, ROWS * j + 1, ROWS, 1), pad_rows(xnp, ROWS * j + 1, ROWS, 1),
                                            pad_rows(xh, ROWS * j + 1, ROWS, 1).bitcast(F32),
                                            ALU.subtract).then_inc(xl_ready, 1)
                with dve.Fori(0, NJ) as j:
                    dve.wait_ge(conv_ready, NJ * g + j + 1)
                    nc.vector.scalar_tensor_tensor(out=xw[:, ds(j * CH, CH)], in0=PS[:, j, 0:CH], scalar=v("bc"),
                                                   in1=xw[:, ds(j * CH, CH)], op0=ALU.add,
                                                   op1=ALU.add).then_inc(l2_done, 1)

                dve.wait_ge(l2_done, NJ * g + NJ)
                stats(3, xw)
                for j in range(NJ):
                    c = slice(j * CH, (j + 1) * CH)
                    dve.wait_ge(part_h, NJ * g + j + 1)
                    if j >= 2:
                        dve.wait_ge(part_l, NJ * g + j - 1)
                    nc.vector.tensor_tensor(rest[:, j % 2, :], PS[0:4 * DK, j, 0:CH], parts[:, 0, c],
                                            ALU.subtract).then_inc(rest_h, 1)
                    if j:
                        low_part(dve, g, j - 1)
                low_part(dve, g, NJ - 1)

                def max_tile(i, sidx):
                    dve.wait_ge(mx_ready, NMAX * sidx + i + 1)
                    nc.vector.reduce_max(nmt[:, i:i + 1], PS[0:BLK, MAXB + i % 2, 0:CH], X,
                                         negate=True).then_inc(mx_free, 1)

                def split_max(sidx):
                    def step(ins, k):
                        ins.then_inc(mxstep, 1)
                        dve.wait_ge(mxstep, 4 * sidx + k)
                    dve.wait_ge(mx_free, NMAX * (sidx + 1) + 2)
                    step(nc.vector.tensor_reduce(nm[:, 0, :], nmt[:, :].rearrange("p (a b) -> p a b", b=NJ), X,
                                                 ALU.min), 1)
                    step(nc.vector.tensor_copy(mp[:, :, 0], nm[:, 0, :]), 2)
                    step(nc.vector.tensor_tensor(nm[:, 1, :], nm[:, 0, :], mp[:, :, 0], ALU.subtract), 3)
                    step(nc.vector.tensor_copy(mp[:, :, 1], nm[:, 1, :]), 4)
                    nc.vector.tensor_tensor(mp[:, :, 2], nm[:, 1, :], mp[:, :, 1], ALU.subtract).then_inc(negm, 1)

                def superblock(sidx, more):
                    for j in range(NQ):
                        if more:
                            for i in max_tiles_at(j):
                                max_tile(i, sidx + 1)
                            if j == LAST_MAX_STEP:
                                split_max(sidx + 1)
                        if j in DVE_SUMS:
                            r = key_rows(j)
                            dve.wait_ge(exp_done, NQ * sidx + j + 1)
                            e = Pb[0:r, j % PSLOTS, :, :]
                            if j == DVE_SUMS[0]:
                                dve.wait_ge(d_ready, sidx + 1)
                                nc.vector.tensor_copy(accD[0:r, :, :], e).then_inc(psum_dve, 1)
                            else:
                                dve.wait_ge(psum_dve, NDVE * (sidx + 1) + dve_sums_upto(j) - 1)
                                nc.vector.tensor_tensor(accD[0:r, :, :], accD[0:r, :, :], e,
                                                        ALU.add).then_inc(psum_dve, 1)
                    dve.wait_ge(d_ready, sidx + 2)
                    dve.wait_ge(fin_done, sidx + 1)
                    nc.vector.reciprocal(Rr[:, :], PS[:, 7, 0:CH]).then_inc(recip, 1)

                for i in range(NMAX):
                    max_tile(i, NJ * g)
                split_max(NJ * g)
                with dve.Fori(0, NJ - 1) as s:
                    superblock(NJ * g + s, True)
                superblock(NJ * g + NJ - 1, False)
                assert n[0] == LINKS, n[0]

        @block.scalar
        def _(act):
            act.sem_inc(pv_done, PSLOTS)
            act.wait_ge(borders, 1)
            with act.Fori(0, GROUPS) as g:
                def normalise(layer, dst, src, done):
                    for j in range(NJ):
                        nc.scalar.activation(dst(j), rows(src[:, j * CH:(j + 1) * CH]), ACT.Identity,
                                             bias=nb[:, :], scale=rstd[:, :]).then_inc(done, 1)

                def padded(t):
                    return lambda j: pad_rows(t, ROWS * j + 1, ROWS, 1)

                act.wait_ge(gn_nb[0], g + 1)
                normalise(0, padded(xnp), xin, xn_ready[0])
                for j in range(NJ):
                    act.wait_ge(sft_ready, NJ * g + j + 1)
                    nc.scalar.activation(rows(SF[:, j * CH:(j + 1) * CH]), pad_rows(sTb[0:3 * PITCH, j, :], 0, ROWS),
                                         ACT.Copy).then_inc(SF_ready, 1)
                act.wait_ge(gn_nb[1], g + 1)
                normalise(1, padded(xnp), xw, xn_ready[1])
                act.wait_ge(U_ready, g + 1)
                for j in range(NJ):
                    act.wait_ge(l1_ps, NJ * g + j + 1)
                    if j >= 2:
                        act.wait_ge(gated_ready, NJ * g + j - 1)
                    nc.scalar.activation(att[:, j % 2, :], PS[:, 3 + j % 3, 0:CH], ACT.Sigmoid,
                                         bias=uc[:, 1:2]).then_inc(att_ready, 1)
                act.wait_ge(gn_nb[2], g + 1)
                for j in range(NJ):
                    src = rows(xw[:, j * CH:(j + 1) * CH])
                    nc.scalar.activation(pad_rows(xh, ROWS * j + 1, ROWS, 1), src, ACT.Identity,
                                         bias=nb[:, :], scale=rstd[:, :])
                    nc.scalar.activation(pad_rows(xnp, ROWS * j + 1, ROWS, 1), src, ACT.Identity,
                                         bias=nb[:, :], scale=rstd[:, :]).then_inc(xn_ready[2], 1)
                act.wait_ge(gn_nb[3], g + 1)
                normalise(3, lambda j: rows(xnf[:, j * CH:(j + 1) * CH]), xw, xn_ready[3])

                def middle_part(j):
                    act.wait_ge(rest_h, NJ * g + j + 1)
                    nc.scalar.activation(parts[:, 1, j * CH:(j + 1) * CH], rest[:, j % 2, :],
                                         ACT.Copy).then_inc(part_m, 1)

                for j in range(NJ):
                    act.wait_ge(qk_ps, NJ * g + j + 1)
                    if j == 0:
                        act.wait_ge(qk_loaded, 16 * (24 * g + 1))
                    nc.scalar.activation(parts[:, 0, j * CH:(j + 1) * CH], PS[0:4 * DK, j, 0:CH],
                                         ACT.Copy).then_inc(part_h, 1)
                    if j:
                        middle_part(j - 1)
                middle_part(NJ - 1)
                for i in range(NJ):
                    m = min(4, NQ - 4 * i)
                    r = key_rows(NQ - 1) if m < 4 else QC
                    act.wait_ge(v_ps, NJ * g + i + 1)
                    nc.scalar.activation(VT[0:r, 4 * i:4 * i + m, :],
                                         PS[0:r, i, 0:m * P].rearrange("p (a b) -> p a b", b=P),
                                         ACT.Copy).then_inc(v_ready, 1)

                def max_rows(sidx, s):
                    act.wait_ge(mrow_ps, sidx + 1)
                    nc.scalar.activation(Qa[KROWS:KROWS + 3, :, ds(s * CH, CH)],
                                         rowb[KROWS:KROWS + 3, 0:2 * CH].rearrange("p (h n) -> p h n", h=2),
                                         ACT.Copy).then_inc(mrow, 1)

                def superblock(sidx, s, more):
                    for j in range(NQ):
                        r = key_rows(j)
                        act.wait_ge(st_ready, NQ * sidx + j + 1)
                        act.wait_ge(pv_done, NQ * sidx + j + 1)
                        i = (j - PSLOTS) % NQ
                        if i in DVE_SUMS:
                            act.wait_ge(psum_dve, NDVE * (sidx + (j >= PSLOTS)) + dve_sums_upto(i))
                        else:
                            act.wait_ge(psum_pool, POOL_SUMS * (sidx + (j >= PSLOTS)) + pool_sums_upto(i))
                        nc.scalar.activation(Pb[0:r, j % PSLOTS, :, :], PS[0:r, 2 * (j % 2):2 * (j % 2) + 2, 0:CH],
                                             ACT.Exp).then_inc(exp_done, 1)
                        if more and j == LAST_MAX_STEP + 2:
                            max_rows(sidx + 1, s + 1)
                    act.wait_ge(pv_done, NQ * (sidx + 1) + PSLOTS)
                    act.wait_ge(fin_done, sidx + 1)
                    nc.scalar.activation(Osb[:, :], PS[:, OB, 0:CH], ACT.Copy).then_inc(ocopy, 1)

                max_rows(NJ * g, 0)
                with act.Fori(0, NJ - 1) as s:
                    superblock(NJ * g + s, s, True)
                superblock(NJ * g + NJ - 1, NJ - 1, False)

        @block.gpsimd
        def _(pool):
            pool.sem_inc(psum_pool, POOL_SUMS)
            pool.sem_inc(pooltaps, 1)
            pool.wait_ge(borders, 1)
            pool.wait_ge(consts, 1)
            STEPS = 2 * NJ
            with pool.Fori(0, GROUPS) as g:
                def power(layer):
                    pool.wait_ge(gn_ve[layer], g + 1)
                    nc.gpsimd.tensor_tensor(rstd[:, :], ve[:, :], mhalf[:, 0:1], ALU.pow).then_inc(gn_rstd[layer], 1)

                power(0)
                pool.wait_ge(yvar_ready, g + 1)
                nc.gpsimd.tensor_tensor(ys[:, 4:5], ys[:, 3:4], phalf[:, 0:1], ALU.pow).then_inc(ysd_ready, 1)
                pool.wait_ge(sfvar_ready, g + 1)
                nc.gpsimd.tensor_tensor(sfs[:, 4, :], sfs[:, 3, :], phalf[0:SP2, 0:2 * NSP],
                                        ALU.pow).then_inc(sfsd_ready, 1)
                with pool.Fori(0, NJ) as j:
                    k = NJ * g + j
                    pool.wait_ge(prod_ready, TAPS * k + 2 + TAP_BANKS)
                    nc.gpsimd.tensor_tensor(pu[:, 0, :], prod[:, 0, :], prod[:, 1, :], ALU.add)
                    pool.wait_ge(prod_ready, TAPS * k + 4 + TAP_BANKS)
                    nc.gpsimd.tensor_tensor(pu[:, 1, :], prod[:, 2, :], prod[:, 3, :], ALU.add).then_inc(pool_step, 1)
                    pool.wait_ge(pool_step, 2 * k + 1)
                    nc.gpsimd.tensor_tensor(pu[:, 0, :], pu[:, 0, :], pu[:, 1, :], ALU.add).then_inc(pool_step, 1)
                    pool.wait_ge(pool_step, 2 * k + 2)
                    pool.wait_ge(l0_done, k + 1)
                    nc.gpsimd.tensor_tensor(pu[:, 2, :], pu[:, 0, :], xin[:, ds(j * CH, CH)],
                                            ALU.add).then_inc(pooltaps, 1)
                power(1)
                power(2)
                power(3)

                def superblock(sidx, s):
                    for j in range(1, NQ):
                        if j in DVE_SUMS:
                            continue
                        pool.wait_ge(exp_done, NQ * sidx + j + 1)
                        if j == 1:
                            pool.wait_ge(d_ready, sidx + 1)
                            nc.gpsimd.tensor_tensor(accP[:, :, :], Pb[:, 0, :, :], Pb[:, 1, :, :],
                                                    ALU.add).then_inc(psum_pool, 2)
                        else:
                            pool.wait_ge(psum_pool, POOL_SUMS * (sidx + 1) + pool_sums_upto(j) - 1)
                            nc.gpsimd.tensor_tensor(accP[:, :, :], accP[:, :, :], Pb[:, j % PSLOTS, :, :],
                                                    ALU.add).then_inc(psum_pool, 1)
                    pool.wait_ge(ocopy, sidx + 2)
                    pool.wait_ge(recip, sidx + 2)
                    nc.gpsimd.tensor_tensor(fin[:, :], Osb[:, :], Rr[:, :], ALU.mult).then_inc(fin_step, 1)
                    pool.wait_ge(fin_step, sidx + 1)
                    nc.gpsimd.tensor_tensor(xw[:, ds(s * CH, CH)], xw[:, ds(s * CH, CH)], fin[:, :],
                                            ALU.add).then_inc(fin_done, 1)

                with pool.Fori(0, NJ) as s:
                    superblock(NJ * g + s, s)

        @block.tensor
        def _(pe):
            mm = nc.tensor.matmul
            pe.sem_inc(accum_ready, 1)
            pe.sem_inc(l0_done, 1)
            pe.wait_ge(consts, 2)
            pe.wait_ge(w_loaded, LOADED)
            with pe.Fori(0, GROUPS) as g:
                def pair_stats(layer):
                    pe.wait_ge(gn_mean[layer], g + 1)
                    mm(small[:, 0:1], pair, mv[:, 0:1], start=True, stop=True).then_inc(gn_pm[layer], 1)
                    pe.wait_ge(gn_sq[layer], g + 1)
                    mm(small[:, 1:2], pair, sq[:, :], start=True, stop=True).then_inc(gn_pv[layer], 1)

                pair_stats(0)
                pe.wait_ge(pooled_ready, 2 * g + 1)
                mm(small[0:2 * MID, 2:3], wcol("w1"), pooled[:, 0:1], start=True, stop=True).then_inc(mid_ready, 1)
                pe.wait_ge(y1_ready, g + 1)
                for t in range(TAPS):
                    last = mm(small[:, 8 + t:9 + t], wcol("w2")[0:2 * MID, t * P:(t + 1) * P], y1[:, :],
                              start=True, stop=True)
                last.then_inc(y_ready, 1)
                pe.wait_ge(xn_ready[0], NJ * (g + 1))
                pe.wait_ge(ocopy, NJ * g + 1)
                for i in range(NSP):
                    last = mm(PS[0:SP2, OB, i * PART:(i + 1) * PART], xnp[:, (2 * i + 1) * PW + 1:(2 * i + 3) * PW + 1], wcol("ws"),
                              start=True, stop=True)
                last.then_inc(sfT_ready, 1)
                pe.wait_ge(sfp_ready, g + 1)
                for j in range(NJ):
                    for i in range(4):
                        last = nc.tensor.transpose(sTb[0:3 * PITCH, j, i * SP2:(i + 1) * SP2],
                                                   sfp[:, 4 * j + i, :, :].rearrange("p a b -> p (a b)"),
                                                   identb[0:SP2, 0:SP2])
                    last.then_inc(sft_ready, 1)

                def spread_tap(j, t):
                    k = NJ * g + j
                    pe.wait_ge(prod_ready, TAPS * k + t + 1)
                    mm(PS[:, t % TAP_BANKS, 0:CH], selb[:, t, :], SF[:, ds(j * CH, CH)],
                       start=True, stop=True).then_inc(tap_ready, 1)

                def add_tap(j, t):
                    k = NJ * g + j
                    pe.wait_ge(prod_ready, TAPS * k + t + 1 + TAP_BANKS)
                    if t == POOL_TAPS:
                        pe.wait_ge(l0_done, k + 1)
                    ins = mm(PS[:, ACCB, 0:CH], identf, prod[:, t, :], start=(t == POOL_TAPS), stop=(t == TAPS - 1))
                    if t == TAPS - 1:
                        ins.then_inc(accum_ready, 1)

                def taps(j, first):
                    for t in range(TAPS):
                        spread_tap(j, t)
                        if t in (1, 2) and not first:
                            add_tap(j - 1, TAPS - 3 + t)
                        if t - 2 >= POOL_TAPS:
                            add_tap(j, t - 2)

                pe.wait_ge(SF_ready, NJ * (g + 1))
                taps(0, True)
                with pe.Fori(1, NJ) as j:
                    taps(j, False)
                add_tap(NJ - 1, TAPS - 2)
                add_tap(NJ - 1, TAPS - 1)

                pair_stats(1)
                pe.wait_ge(pooled_ready, 2 * g + 2)
                mm(small[0:2 * CR, 20:21], wcol("wk"), pooled[:, 1:2], start=True, stop=True).then_inc(km_ps, 1)
                pe.wait_ge(km_ready, g + 1)
                mm(small[:, 21:22], wcol("wq")[0:2 * CR], km[:, 0:1], start=True, stop=True)
                mm(small[:, 22:23], half8[0:2 * CR], km[:, 1:2], start=True, stop=True).then_inc(u_ps, 1)
                for j in range(NJ):
                    pe.wait_ge(xn_ready[1], NJ * g + j + 1)
                    if j == 0:
                        pe.wait_ge(U_ready, g + 1)
                    if j >= 3:
                        pe.wait_ge(gated_ready, NJ * g + j - 2)
                    xnj = pad_rows(xnp, ROWS * j + 1, ROWS, 1)
                    mm(PS[:, j % 3, 0:CH], wcol("wv"), xnj, start=True, stop=True)
                    mm(PS[:, 3 + j % 3, 0:CH], U[:, :], xnj, start=True, stop=True).then_inc(l1_ps, 1)

                pair_stats(2)
                with pe.Fori(0, NJ) as j:
                    pe.wait_ge(xl_ready, NJ * (g + 1))
                    for src in (xh, xl):
                        for t in range(TAPS):
                            last = mm(PS[:, j, 0:CH], wt[:, t * P:(t + 1) * P],
                                      pad_rows_at(src, j * (ROWS * PW) + (t // 3) * PW + t % 3, ROWS),
                                      start=(src is xh and t == 0), stop=(src is xl and t == TAPS - 1))
                    last.then_inc(conv_ready, 1)

                pair_stats(3)
                for j in range(NJ):
                    pe.wait_ge(xn_ready[3], NJ * g + j + 1)
                    mm(PS[0:4 * DK, j, 0:CH], wcol("qk3"), xnf[:, j * CH:(j + 1) * CH],
                       start=True, stop=True).then_inc(qk_ps, 1)
                for j in range(NQ):
                    r = key_rows(j)
                    if j % 4 == 0:
                        pe.wait_ge(rest_h, NJ * g + j // 4 + 1)
                    last = mm(PS[0:r, j // 4, (j % 4) * P:(j % 4 + 1) * P], xnf[:, j * QC:j * QC + r], wcol("wv3"),
                              start=True, stop=True)
                    if j % 4 == 3 or j == NQ - 1:
                        last.then_inc(v_ps, 1)

                def max_tile(i, sidx, s):
                    h, blk, t = i // (4 * NJ), i // NJ % 4, i % NJ
                    pe.wait_ge(mx_free, NMAX * sidx + i + 1)
                    mm(PS[0:BLK, MAXB + i % 2, 0:CH], Qa[0:KROWS, h, ds(s * CH + blk * BLK, BLK)],
                       Ka[0:KROWS, h, t * CH:(t + 1) * CH], start=True, stop=True).then_inc(mx_ready, 1)

                def max_rows(sidx):
                    pe.wait_ge(negm, sidx + 1)
                    for i in range(8):
                        last = nc.tensor.transpose(rowb[KROWS:KROWS + 3, i * BLK:(i + 1) * BLK], mp[:, i, :],
                                                   identb[0:BLK, 0:BLK])
                    last.then_inc(mrow_ps, 1)

                def scores(j, s):
                    r = key_rows(j)
                    for h in range(2):
                        last = mm(PS[0:r, 2 * (j % 2) + h, 0:CH], Ka[0:KROWS + 3, h, j * QC:j * QC + r],
                                  Qa[0:KROWS + 3, h, ds(s * CH, CH)], start=True, stop=True)
                    last.then_inc(st_ready, 1)

                def superblock(sidx, s, more):
                    for j in range(NQ):
                        pe.wait_ge(exp_done, NQ * sidx + j + 1)
                        if j == 0:
                            pe.wait_ge(ocopy, sidx + 1)
                        for h in range(2):
                            last = mm(PS[C * h:C * h + C, OB, 0:CH], VT[:, j, C * h:C * h + C],
                                      Pb[:, j % PSLOTS, h, :], start=(j == 0), stop=(j == NQ - 1))
                        last.then_inc(pv_done, 1)
                        if j < NQ - 2:
                            scores(j + 2, s)
                        if more:
                            for i in max_tiles_at(j):
                                max_tile(i, sidx + 1, s + 1)
                            if j == LAST_MAX_STEP + 1:
                                pe.wait_ge(recip, sidx + 1)
                                max_rows(sidx + 1)
                    if more:
                        pe.wait_ge(mrow, sidx + 2)
                        scores(0, s + 1)
                        scores(1, s + 1)
                    pe.wait_ge(psum_pool, POOL_SUMS * (sidx + 2))
                    pe.wait_ge(psum_dve, NDVE * (sidx + 2))
                    for h in range(2):
                        mm(PS[C * h:C * h + C, 7, 0:CH], ones[:, :], accP[:, h, :], start=True, stop=False)
                        last = mm(PS[C * h:C * h + C, 7, 0:CH], ones[:, :], accD[:, h, :], start=False, stop=True)
                    last.then_inc(d_ready, 1)

                pe.wait_ge(v_ready, NJ * (g + 1))
                pe.wait_ge(qk_loaded, 16 * (24 * (g + 1) + 1))
                for i in range(NMAX):
                    max_tile(i, NJ * g, 0)
                max_rows(NJ * g)
                pe.wait_ge(mrow, NJ * g + 1)
                scores(0, 0)
                scores(1, 0)
                with pe.Fori(0, NJ - 1) as s:
                    superblock(NJ * g + s, s, True)
                superblock(NJ * g + NJ - 1, NJ - 1, False)


def constants(np):
    c = np.zeros((P, CCOLS), np.float32)
    p = np.arange(P)
    c[:, 0:P] = np.eye(P)
    c[:, P:2 * P] = 0.5 * (p[:, None] // 2 == p[None, :] // 2)
    c[:, 2 * P:3 * P] = p[:, None] // C == p[None, :] // C
    c[0:2 * CR, 3 * P:4 * P] = p[0:2 * CR, None] // CR == p[None, :] // C
    for part in range(3):
        for h in range(2):
            for t in range(TAPS):
                a = 4 * P + t * P + C * h
                c[part * PITCH + h * TAPS + t, a:a + C] = 1.0
    return c


def kernel(**inputs):
    import numpy as np
    import concourse.bacc as bacc
    from concourse.bass_utils import run_bass_kernel_spmd

    a = {k: np.asarray(w) for k, w in inputs.items()}
    arrays = {
        "x": a["x"].reshape(GROUPS, P, HW),
        "w1t": a["L0_conv_w1"].T, "b1": a["L0_conv_b1"].reshape(MID, 1),
        "w2t": a["L0_conv_w2"].reshape(C, TAPS, MID).transpose(2, 1, 0),
        "b2": a["L0_conv_b2"].reshape(C, TAPS),
        "wst": a["L0_conv_ws"].T, "bs": a["L0_conv_bs"], "fn": a["L0_conv_fn_std"].reshape(C, TAPS),
        "wq": a["L1_conv_Wq"], "bq": a["L1_conv_bq"].reshape(CR, 1),
        "wkt": a["L1_conv_Wk"].T, "bk": a["L1_conv_bk"].reshape(CR, 1),
        "wvt": a["L1_conv_Wv"].T, "bv": a["L1_conv_bv"].reshape(C, 1),
        "wc": a["L2_conv_weight"].transpose(1, 2, 3, 0).reshape(C, TAPS, C),
        "bc": a["L2_conv_bias"].reshape(C, 1),
        "q3t": a["L3_conv_q_w"].T, "k3t": a["L3_conv_k_w"].T, "v3t": a["L3_conv_v_w"].T,
        "cst": constants(np),
    }
    nc = bacc.Bacc("TRN2", target_bir_lowering=False, num_devices=1)
    arrays = {f"in_{k}": np.ascontiguousarray(w) for k, w in arrays.items()}
    args = [nc.dram_tensor(k, w.shape, mybir.dt.from_np(w.dtype), kind="ExternalInput").ap()
            for k, w in arrays.items()]
    out = nc.dram_tensor("out", (GROUPS, P, HW), F32, kind="ExternalOutput").ap()
    build(nc, *args, out)
    r = run_bass_kernel_spmd(nc, [arrays], core_ids=[0])
    return r.results[0]["out"].reshape(B, C, H, W)
```

```python
from contextlib import ExitStack

import concourse.bass as bass
from concourse import mybir

F32 = mybir.dt.float32
F32R = mybir.dt.float32r
BF16 = mybir.dt.bfloat16
ALU = mybir.AluOpType
ACT = mybir.ActivationFunctionType
X = mybir.AxisListType.X
ds = bass.ds

B, C, H, W = 8, 64, 56, 56
P = 2 * C
GROUPS = B // 2
HW = H * W
ROWS = 8
CH = ROWS * W
NJ = HW // CH
PW = W + 2
PADDED = PW * (H + 2) + 4
TAPS = 9
MID = 12
CR = 8
DK = 16
GAIN_OVER_K = float(2.0 ** 0.5) / 3
THRESHOLD = 0.05
SP2 = 2 * PW
NSP = H // 2
PART = 2 * TAPS
PITCH = 32
QC = 128
NQ = -(-HW // QC)
KROWS = 6 * DK
QUART = CH // 4
BLK = 128
HWQ = -(-HW // BLK) * BLK
FINISH_STEP = 3
TILES = 2 * NJ
FIRST_TILES, PAIR_TILES = 4 * TILES, 7 * TILES
GROUP_TILES = FIRST_TILES + (NJ // 2) * PAIR_TILES
PSLOTS = 5
TAP_BANKS = 3
POOL_TAPS = 4
DVE_SUMS = (3, 7, 11, 15, 19, 23, 24)
TURN = 7
TO_ACCP = 5
SPLIT_STEP = 19
ROWS_STEP = 21
FREE7 = range(8, SPLIT_STEP)


def plan_tiles():
    n, plan, held = SPLIT_STEP + 1, [], {4: 0, 5: 0, 7: 0}
    early, late = 3 * TILES, PAIR_TILES - 3 * TILES
    over = late - early
    steps = [i * n // early for i in range(early)]
    steps += [n + i * (NQ - n) // over for i in range(over)]
    steps += [NQ + i * n // (late - over) for i in range(late - over)]
    for i, step in enumerate(steps):
        banks = (4, 5, 7) if step % NQ in FREE7 else (4, 5)
        bank = min(banks, key=lambda b: held[b])
        plan.append((step, bank, held[bank]))
        held[bank] = i + 1
    return plan


PLAN = plan_tiles()

COLS = {}
_at = 0
for _name, _n in (("w1", 2 * MID), ("ws", PART), ("wv", P), ("wk", 2 * CR), ("qk3", 4 * DK), ("wv3", P),
                  ("w2", TAPS * P), ("wq", P), ("conv", TAPS * P)):
    COLS[_name] = (_at, _at + _n)
    _at += _n
WCOLS = _at
VEC = {"b2": (0, 9), "fn": (9, 18), "b1": (18, 19), "bk": (19, 20), "bq": (20, 21), "bv": (21, 22),
       "bc": (22, 23), "bs": (23, 32)}
VCOLS = 32
CST = {"ident": (0, P), "pair": (P, 2 * P), "half": (2 * P, 3 * P), "half8": (3 * P, 4 * P),
       "sel": (4 * P, (4 + TAPS) * P)}
CCOLS = (4 + TAPS) * P


def key_rows(j):
    return min(QC, HW - j * QC)


def pool_sums_upto(j):
    return sum(1 for i in range(max(j, 1) + 1) if i not in DVE_SUMS)


def dve_sums_upto(j):
    return sum(1 for i in range(j + 1) if i in DVE_SUMS)


POOL_SUMS = pool_sums_upto(NQ - 1)
NDVE = len(DVE_SUMS)


def tiles_at(step):
    return [i for i, (at, _, _) in enumerate(PLAN) if at == step]


def build(nc, x, w1t, b1, w2t, b2, wst, bs, fn, wq, bq, wkt, bk, wvt, bv, wc, bc, q3t, k3t, v3t, cst, out):
    with ExitStack() as ctx:
        def sb(name, shape, dt=F32):
            return ctx.enter_context(nc.sbuf_tensor(name, shape, dt))

        def sem(name):
            return ctx.enter_context(nc.semaphore(name))

        xin = sb("xin", [P, HW])
        xw = sb("xw", [P, HW])
        xnp = sb("xnp", [P, PADDED])
        xh = sb("xh", [P, PADDED], F32R)
        xl = sb("xl", [P, PADDED], F32R)
        xnf = sb("xnf", [P, HW])
        wz = sb("wz", [P, WCOLS])
        wt = sb("wt", [P, TAPS * P], F32R)
        vec = sb("vec", [P, VCOLS])
        cs = sb("cs", [P, CCOLS])
        selb = sb("selb", [3 * PITCH, TAPS, P], BF16)
        identb = sb("identb", [P, P], BF16)
        ones = sb("ones", [P, C])
        mhalf = sb("mhalf", [P, 64])
        phalf = sb("phalf", [P, 64])
        st6 = sb("st6", [P, NJ, 6])
        mv = sb("mv", [P, 2])
        idle = sb("idle", [P, 1])
        dm = sb("dm", [P, 1])
        sq = sb("sq", [P, 1])
        ve = sb("ve", [P, 1])
        rstd = sb("rstd", [P, 1])
        nb = sb("nb", [P, 1])
        pooled = sb("pooled", [P, 2])
        y1 = sb("y1", [2 * MID, 1])
        yf = sb("yf", [P, TAPS])
        ysq = sb("ysq", [P, TAPS])
        ys = sb("ys", [P, 6])
        cf = sb("cf", [P, TAPS])
        sf = sb("sf", [SP2, NSP * 2, TAPS])
        sf2 = sb("sf2", [SP2, NSP * 2, TAPS])
        sfs = sb("sfs", [SP2, 5, NSP * 2])
        sfp = sb("sfp", [SP2, NSP, 3, PITCH], BF16)
        km = sb("km", [2 * CR, 2])
        uc = sb("uc", [P, 2])
        U = sb("U", [P, P])
        parts = sb("parts", [4 * DK, 3, HW], BF16)
        rest = sb("rest", [4 * DK, 2, CH])
        Qa = sb("Qa", [P, 2, HWQ], BF16)
        Ka = sb("Ka", [P, 2, HW], BF16)
        VT = sb("VT", [QC, NQ, P])
        Pb = sb("Pb", [QC, PSLOTS, 2, CH])
        flat = Pb[:, :, :, :].rearrange("p a b c -> p (a b c)")
        tneg = flat[:, 0:TAPS * P]
        prod = flat[:, 0:TAPS * CH].rearrange("p (t n) -> p t n", t=TAPS)
        flat = VT[:, :, :].rearrange("p a b -> p (a b)")
        pu = flat[:, 0:3 * CH].rearrange("p (a n) -> p a n", a=3)
        SF = Qa[0:3 * PITCH, 0, 0:HW]
        accP = sb("accP", [QC, 2, CH])
        accQ = sb("accQ", [QC, 2, CH])
        accD = sb("accD", [QC, 2, CH])
        att, gated = accP, accD
        nmt = sb("nmt", [BLK, PAIR_TILES // NJ, NJ])
        nm = sb("nm", [BLK, 2, 8])
        mp = sb("mp", [BLK, 8, 3], BF16)
        Osb = sb("Osb", [P, CH])
        Rr = sb("Rr", [P, CH])
        fin = sb("fin", [P, CH])

        PS = ctx.enter_context(nc.psum_tensor("PS", [P, 8, 512], F32))
        small = PS[:, 7, :]
        ACCB = 4
        OB = 6
        sTb = PS[:, 0:NJ, :].bitcast(BF16)
        rowb = PS[:, 7, :].bitcast(BF16)

        def pad_rows(t, r0, n, c0=0):
            return t[:, r0 * PW + c0:(r0 + n) * PW + c0].rearrange("p (r w) -> p r w", w=PW)[:, :, 0:W]

        def pad_rows_at(t, off, n):
            return t[:, ds(off, n * PW)].rearrange("p (r w) -> p r w", w=PW)[:, :, 0:W]

        def rows(ap):
            return ap.rearrange("p (r w) -> p r w", w=W)

        def wcol(name):
            return wz[:, COLS[name][0]:COLS[name][1]]

        def v(name, n=P):
            return vec[0:n, VEC[name][0]:VEC[name][1]]

        identf = cs[:, CST["ident"][0]:CST["ident"][1]]
        pair = cs[:, CST["pair"][0]:CST["pair"][1]]
        halfm = cs[:, CST["half"][0]:CST["half"][1]]
        half8 = cs[:, CST["half8"][0]:CST["half8"][1]]

        zeroed = sem("weights_zeroed")
        w_loaded = sem("weights_loaded")
        borders = sem("borders_zeroed")
        consts = sem("constants_ready")
        x_loaded = sem("x_loaded")
        dve_step = sem("dve_step")
        gn_mean = [sem(f"gn_mean_{i}") for i in range(4)]
        gn_pm = [sem(f"gn_pair_mean_{i}") for i in range(4)]
        gn_sq = [sem(f"gn_squares_{i}") for i in range(4)]
        gn_pv = [sem(f"gn_pair_var_{i}") for i in range(4)]
        gn_ve = [sem(f"gn_var_eps_{i}") for i in range(4)]
        gn_rstd = [sem(f"gn_rstd_{i}") for i in range(4)]
        gn_nb = [sem(f"gn_bias_{i}") for i in range(4)]
        pooled_ready = sem("pooled_ready")
        xn_ready = [sem(f"xn_ready_{i}") for i in range(4)]
        mid_ready = sem("mid_ready")
        y1_ready = sem("y1_ready")
        y_ready = sem("y_ready")
        yvar_ready = sem("yvar_ready")
        ysd_ready = sem("ysd_ready")
        sfT_ready = sem("sfT_ready")
        sfvar_ready = sem("sfvar_ready")
        sfsd_ready = sem("sfsd_ready")
        sfp_ready = sem("sf_parts_ready")
        sft_ready = sem("sf_transposed")
        SF_ready = sem("SF_ready")
        tap_ready = sem("tap_ready")
        prod_ready = sem("prod_ready")
        accum_ready = sem("tap_sum_ready")
        pool_step = sem("pool_step")
        pooltaps = sem("pool_taps_summed")
        l0_done = sem("l0_chunk_done")
        km_ps = sem("km_in_psum")
        km_ready = sem("km_ready")
        u_ps = sem("u_in_psum")
        U_ready = sem("U_ready")
        l1_ps = sem("l1_in_psum")
        att_ready = sem("att_ready")
        gated_ready = sem("gated_ready")
        l1_done = sem("l1_chunk_done")
        xh_ready = sem("xh_ready")
        xl_ready = sem("xl_ready")
        conv_ready = sem("conv_ready")
        l2_done = sem("l2_chunk_done")
        qk_ps = sem("qk_in_psum")
        part_h = sem("qk_part_high")
        rest_h = sem("qk_rest")
        part_m = sem("qk_part_middle")
        part_l = sem("qk_part_low")
        qk_loaded = sem("qk_rows_loaded")
        v_ps = sem("v_in_psum")
        v_ready = sem("v_ready")
        mx_ready = sem("max_scores_ready")
        mx_free = sem("max_bank_free")
        mxstep = sem("max_split_step")
        negm = sem("negmax_parts_ready")
        mrow_ps = sem("max_rows_in_psum")
        mrow = sem("max_rows_ready")
        st_ready = sem("scores_ready")
        exp_done = sem("exp_done")
        pv_done = sem("pv_done")
        psum_pool = sem("exps_summed_by_pool")
        psum_dve = sem("exps_summed_by_dve")
        ocopy = sem("output_copied")
        d_ready = sem("denominators_ready")
        recip = sem("reciprocals_ready")
        fin_step = sem("normalised")
        fin_done = sem("l3_chunk_done")
        stored = sem("stored")

        loads = []
        for h in range(2):
            cc = slice(C * h, C * h + C)

            def blk(name, a, n, p=cc):
                return wz[p, COLS[name][0] + a:COLS[name][0] + a + n]
            loads += [
                (blk("w1", MID * h, MID), w1t), (blk("ws", TAPS * h, TAPS), wst), (blk("wv", C * h, C), wvt),
                (blk("wk", CR * h, CR), wkt), (blk("qk3", 2 * DK * h, DK), q3t),
                (blk("qk3", 2 * DK * h + DK, DK), k3t), (blk("wv3", C * h, C), v3t),
                (blk("wq", C * h, C, slice(CR * h, CR * h + CR)), wq),
                (wz[MID * h:MID * h + MID, COLS["w2"][0]:COLS["w2"][1]]
                 .rearrange("m (t c) -> m t c", t=TAPS)[:, :, cc], w2t),
                (wcol("conv")[cc].rearrange("m (t c) -> m t c", t=TAPS)[:, :, cc], wc),
                (v("b2")[cc], b2), (v("fn")[cc], fn), (v("bv")[cc], bv), (v("bc")[cc], bc),
                (vec[MID * h:MID * h + MID, 18:19], b1), (vec[CR * h:CR * h + CR, 19:20], bk),
                (vec[CR * h:CR * h + CR, 20:21], bq),
            ]
        loads += [(cs[:, :], cst), (v("bs"), bs.partition_broadcast(P))]
        LOADED = 16 * len(loads)
        LINKS = 31

        block = ctx.enter_context(nc.Block())

        @block.sync
        def _(sp):
            sp.dma_start(xin[:, :], x[0]).then_inc(x_loaded, 16)
            sp.sem_inc(stored, 16)
            sp.sem_inc(qk_loaded, 16)
            for first in (ocopy, d_ready, recip, fin_done):
                sp.sem_inc(first, 1)
            sp.wait_ge(zeroed, 1)
            for dst, src in loads:
                sp.dma_start(dst, src).then_inc(w_loaded, 16)

            def spread():
                for h in range(2):
                    for dst, base, order in ((Qa, 2 * DK * h, (0, 0, 1, 0, 2, 1)),
                                             (Ka, 2 * DK * h + DK, (0, 1, 0, 2, 0, 1))):
                        for r, part in enumerate(order):
                            sp.dma_start(dst[DK * r:DK * r + DK, h, 0:HW],
                                         parts[base:base + DK, part, :]).then_inc(qk_loaded, 16)

            def store(g):
                with sp.Fori(0, NJ) as s:
                    sp.wait_ge(fin_done, NJ * g + s + 2)
                    sp.dma_start(out[g][:, ds(s * CH, CH)], xw[:, ds(s * CH, CH)]).then_inc(stored, 16)

            def group(g, last):
                sp.wait_ge(part_l, NJ * g + NJ)
                spread()
                if not last:
                    sp.dma_start(xin[:, :], x[g + 1]).then_inc(x_loaded, 16)
                store(g)

            with sp.Fori(0, GROUPS - 1) as g:
                group(g, False)
            group(GROUPS - 1, True)
            sp.wait_ge(stored, 16 * (NJ * GROUPS + 1))

        def low_part(dve, g, j):
            c = slice(j * CH, (j + 1) * CH)
            dve.wait_ge(part_m, NJ * g + j + 1)
            nc.vector.tensor_tensor(parts[:, 2, c], rest[:, j % 2, :], parts[:, 1, c],
                                    ALU.subtract).then_inc(part_l, 1)

        @block.vector
        def _(dve):
            nc.vector.memset(wz[:, :], 0.0)
            nc.vector.memset(vec[:, :], 0.0).then_inc(zeroed, 1)
            nc.vector.memset(xnp[:, :], 0.0)
            nc.vector.memset(xh[:, :].bitcast(F32), 0.0)
            nc.vector.memset(xl[:, :].bitcast(F32), 0.0).then_inc(borders, 1)
            nc.vector.memset(ones[:, :], 1.0)
            nc.vector.memset(sfp[:, :, :, :], 0.0)
            nc.vector.memset(Qa[:, :, HW:HWQ], 0.0)
            nc.vector.memset(mhalf[:, :], -0.5)
            nc.vector.memset(VT[key_rows(NQ - 1):QC, NQ - 1, :], 0.0)
            nc.vector.memset(phalf[:, :], 0.5)
            nc.vector.memset(Ka[KROWS:KROWS + 3, :, :], 1.0)
            dve.sem_inc(prod_ready, TAP_BANKS)
            dve.sem_inc(mx_free, 1)
            dve.sem_inc(psum_dve, NDVE)
            dve.wait_ge(w_loaded, LOADED)
            nc.vector.tensor_copy(selb[:, :, :], cs[0:3 * PITCH, CST["sel"][0]:CST["sel"][1]]
                                  .rearrange("p (t c) -> p t c", t=TAPS))
            nc.vector.tensor_copy(identb[:, :], identf)
            nc.vector.tensor_scalar(tneg, wcol("conv"), -THRESHOLD, None, ALU.is_lt)
            nc.vector.tensor_scalar(wcol("conv"), wcol("conv"), THRESHOLD, None, ALU.is_gt).then_inc(consts, 1)
            dve.wait_ge(consts, 1)
            nc.vector.tensor_tensor(wt[:, :], wcol("conv"), tneg, ALU.subtract).then_inc(consts, 1)

            with dve.Fori(0, GROUPS) as g:
                n = [0]

                def link(ins):
                    n[0] += 1
                    ins.then_inc(dve_step, 1)
                    dve.wait_ge(dve_step, LINKS * g + n[0])

                def stats(layer, src):
                    for i in range(NJ):
                        last = nc.vector.bn_stats(st6[:, i, :], src[:, i * CH:(i + 1) * CH])
                    link(last)
                    nc.vector.memset(idle[:, :], 0.0)
                    nc.vector.bn_aggr(mv[:, :], st6[:, :, :].rearrange("p a b -> p (a b)")).then_inc(gn_mean[layer], 1)
                    dve.wait_ge(gn_pm[layer], g + 1)
                    link(nc.vector.tensor_tensor(dm[:, :], mv[:, 0:1], small[:, 0:1], ALU.subtract))
                    nc.vector.scalar_tensor_tensor(out=sq[:, :], in0=dm[:, :], scalar=dm[:, :], in1=mv[:, 1:2],
                                                   op0=ALU.mult, op1=ALU.add).then_inc(gn_sq[layer], 1)
                    dve.wait_ge(gn_pv[layer], g + 1)
                    nc.vector.tensor_scalar(ve[:, :], small[:, 1:2], 1e-5, None, ALU.add).then_inc(gn_ve[layer], 1)
                    dve.wait_ge(gn_rstd[layer], g + 1)
                    nc.vector.scalar_tensor_tensor(out=nb[:, :], in0=small[:, 0:1], scalar=-1.0, in1=rstd[:, :],
                                                   op0=ALU.mult, op1=ALU.mult).then_inc(gn_nb[layer], 1)

                dve.wait_ge(x_loaded, 16 * g + 16)
                stats(0, xin)
                nc.vector.tensor_tensor(pooled[:, 0:1], dm[:, :], rstd[:, :], ALU.mult).then_inc(pooled_ready, 1)
                dve.wait_ge(mid_ready, g + 1)
                nc.vector.tensor_scalar(y1[:, :], small[0:2 * MID, 2:3], v("b1", 2 * MID), 0.0,
                                        ALU.add, ALU.max).then_inc(y1_ready, 1)
                dve.wait_ge(y_ready, g + 1)
                link(nc.vector.tensor_tensor(yf[:, :], small[:, 8:8 + TAPS], v("b2"), ALU.add))
                link(nc.vector.reduce_sum(ys[:, 0:1], yf[:, :], X))
                link(nc.vector.tensor_scalar(ys[:, 1:2], ys[:, 0:1], 1.0 / TAPS, None, ALU.mult))
                link(nc.vector.tensor_scalar(yf[:, :], yf[:, :], ys[:, 1:2], None, ALU.subtract))
                link(nc.vector.tensor_tensor(ysq[:, :], yf[:, :], yf[:, :], ALU.mult))
                link(nc.vector.reduce_sum(ys[:, 2:3], ysq[:, :], X))
                nc.vector.tensor_scalar(ys[:, 3:4], ys[:, 2:3], 1.0 / (TAPS - 1), None, ALU.mult).then_inc(yvar_ready, 1)
                dve.wait_ge(ysd_ready, g + 1)
                link(nc.vector.tensor_scalar(ys[:, 5:6], ys[:, 4:5], 1e-10, None, ALU.add))
                link(nc.vector.reciprocal(ys[:, 0:1], ys[:, 5:6]))
                link(nc.vector.scalar_tensor_tensor(out=cf[:, :], in0=yf[:, :], scalar=ys[:, 0:1], in1=v("fn"),
                                                    op0=ALU.mult, op1=ALU.mult))

                def per_pixel(i):
                    return sfs[:, i, :].unsqueeze(2).to_broadcast([SP2, 2 * NSP, TAPS])

                dve.wait_ge(sfT_ready, g + 1)
                link(nc.vector.tensor_tensor(
                    sf[:, :, :], PS[0:SP2, OB, 0:2 * NSP * TAPS].rearrange("p (n t) -> p n t", t=TAPS),
                    v("bs", SP2).unsqueeze(1).to_broadcast([SP2, 2 * NSP, TAPS]), ALU.add))
                link(nc.vector.reduce_sum(sfs[:, 0, :], sf[:, :, :], X))
                link(nc.vector.tensor_scalar(sfs[:, 1, :], sfs[:, 0, :], 1.0 / TAPS, None, ALU.mult))
                link(nc.vector.tensor_tensor(sf[:, :, :], sf[:, :, :], per_pixel(1), ALU.subtract))
                link(nc.vector.tensor_tensor(sf2[:, :, :], sf[:, :, :], sf[:, :, :], ALU.mult))
                link(nc.vector.reduce_sum(sfs[:, 2, :], sf2[:, :, :], X))
                nc.vector.tensor_scalar(sfs[:, 3, :], sfs[:, 2, :], 1.0 / (TAPS - 1), None,
                                        ALU.mult).then_inc(sfvar_ready, 1)
                dve.wait_ge(sfsd_ready, g + 1)
                link(nc.vector.tensor_scalar(sfs[:, 0, :], sfs[:, 4, :], 1e-10, None, ALU.add))
                link(nc.vector.reciprocal(sfs[:, 2, :], sfs[:, 0, :]))
                link(nc.vector.scalar_tensor_tensor(out=sf[:, :, :], in0=sf[:, :, :], scalar=GAIN_OVER_K,
                                                    in1=per_pixel(2), op0=ALU.mult, op1=ALU.mult))
                sfv = sf[:, :, :].rearrange("p (n b) t -> p n (b t)", b=2)
                sf2v = sf2[:, :, :].rearrange("p (n b) t -> p n (b t)", b=2)
                link(nc.vector.tensor_copy(sfp[:, :, 0, 0:PART], sfv))
                link(nc.vector.tensor_tensor(sf2v, sfv, sfp[:, :, 0, 0:PART], ALU.subtract))
                link(nc.vector.tensor_copy(sfp[:, :, 1, 0:PART], sf2v))
                nc.vector.tensor_tensor(sfp[:, :, 2, 0:PART], sf2v, sfp[:, :, 1, 0:PART], ALU.subtract).then_inc(sfp_ready, 1)

                def tap(j, t):
                    k = NJ * g + j
                    dve.wait_ge(tap_ready, TAPS * k + t + 1)
                    if t < POOL_TAPS:
                        dve.wait_ge(pool_step, 2 * k + 1)
                    else:
                        dve.wait_ge(accum_ready, k + 1)
                    nc.vector.scalar_tensor_tensor(
                        out=rows(prod[:, t, :]), in0=rows(PS[:, t % TAP_BANKS, 0:CH]), scalar=cf[:, t:t + 1],
                        in1=pad_rows_at(xnp, j * (ROWS * PW) + (t // 3) * PW + t % 3, ROWS),
                        op0=ALU.mult, op1=ALU.mult).then_inc(prod_ready, 1)

                def l0_sum(j):
                    dve.wait_ge(accum_ready, NJ * g + j + 2)
                    dve.wait_ge(pooltaps, NJ * g + j + 2)
                    nc.vector.tensor_tensor(xw[:, ds(j * CH, CH)], PS[:, ACCB, 0:CH], pu[:, 2, :],
                                            ALU.add).then_inc(l0_done, 1)

                dve.wait_ge(stored, 16 * (NJ * g + 1))
                for t in range(TAPS):
                    tap(0, t)
                with dve.Fori(1, NJ) as j:
                    for t in range(TAPS):
                        if t == POOL_TAPS:
                            l0_sum(j - 1)
                        tap(j, t)
                l0_sum(NJ - 1)

                dve.wait_ge(l0_done, NJ * g + NJ + 1)
                stats(1, xw)
                nc.vector.tensor_tensor(pooled[:, 1:2], dm[:, :], rstd[:, :], ALU.mult).then_inc(pooled_ready, 1)
                dve.wait_ge(km_ps, g + 1)
                link(nc.vector.tensor_tensor(km[:, 0:1], small[0:2 * CR, 20:21], v("bk", 2 * CR), ALU.add))
                nc.vector.tensor_tensor(km[:, 1:2], km[:, 0:1], v("bq", 2 * CR), ALU.mult).then_inc(km_ready, 1)
                dve.wait_ge(u_ps, g + 1)
                link(nc.vector.tensor_copy(uc[:, :], small[:, 21:23]))
                nc.vector.tensor_scalar(U[:, :], halfm, uc[:, 0:1], None, ALU.mult).then_inc(U_ready, 1)

                def l1_add(j):
                    dve.wait_ge(gated_ready, NJ * g + j + 1)
                    nc.vector.tensor_tensor(xw[:, j * CH:(j + 1) * CH], xw[:, j * CH:(j + 1) * CH],
                                            gated[:, j % 2, :], ALU.add).then_inc(l1_done, 1)

                for j in range(NJ):
                    dve.wait_ge(att_ready, NJ * g + j + 1)
                    if j >= 2:
                        dve.wait_ge(l1_done, NJ * g + j - 1)
                    nc.vector.scalar_tensor_tensor(out=gated[:, j % 2, :], in0=PS[:, j % 3, 0:CH], scalar=v("bv"),
                                                   in1=att[:, j % 2, :], op0=ALU.add,
                                                   op1=ALU.mult).then_inc(gated_ready, 1)
                    if j:
                        l1_add(j - 1)
                l1_add(NJ - 1)

                dve.wait_ge(l1_done, NJ * g + NJ)
                stats(2, xw)
                for j in range(NJ):
                    dve.wait_ge(xn_ready[2], NJ * g + j + 1)
                    nc.vector.tensor_tensor(pad_rows(xl, ROWS * j + 1, ROWS, 1), pad_rows(xnp, ROWS * j + 1, ROWS, 1),
                                            pad_rows(xh, ROWS * j + 1, ROWS, 1).bitcast(F32),
                                            ALU.subtract).then_inc(xl_ready, 1)
                with dve.Fori(0, NJ) as j:
                    dve.wait_ge(conv_ready, NJ * g + j + 1)
                    nc.vector.scalar_tensor_tensor(out=xw[:, ds(j * CH, CH)], in0=PS[:, j, 0:CH], scalar=v("bc"),
                                                   in1=xw[:, ds(j * CH, CH)], op0=ALU.add,
                                                   op1=ALU.add).then_inc(l2_done, 1)

                dve.wait_ge(l2_done, NJ * g + NJ)
                stats(3, xw)
                for j in range(NJ):
                    c = slice(j * CH, (j + 1) * CH)
                    dve.wait_ge(part_h, NJ * g + j + 1)
                    if j >= 2:
                        dve.wait_ge(part_l, NJ * g + j - 1)
                    nc.vector.tensor_tensor(rest[:, j % 2, :], PS[0:4 * DK, j, 0:CH], parts[:, 0, c],
                                            ALU.subtract).then_inc(rest_h, 1)
                    if j:
                        low_part(dve, g, j - 1)
                low_part(dve, g, NJ - 1)

                def max_tile(i, base, bank):
                    dve.wait_ge(mx_ready, base + i + 1)
                    nc.vector.reduce_max(nmt[:, i // NJ, i % NJ:i % NJ + 1], PS[0:BLK, bank, 0:CH], X,
                                         negate=True).then_inc(mx_free, 1)

                def split_max(sidx, tiles, a, n):
                    def step(ins, k):
                        ins.then_inc(mxstep, 1)
                        dve.wait_ge(mxstep, 4 * sidx + k)
                    dve.wait_ge(mx_free, tiles + 1)
                    m, rest_ = nm[:, 0, 0:n], nm[:, 1, 0:n]
                    step(nc.vector.tensor_reduce(m, nmt[:, a:a + n, :], X, ALU.min), 1)
                    step(nc.vector.tensor_copy(mp[:, 0:n, 0], m), 2)
                    step(nc.vector.tensor_tensor(rest_, m, mp[:, 0:n, 0], ALU.subtract), 3)
                    step(nc.vector.tensor_copy(mp[:, 0:n, 1], rest_), 4)
                    nc.vector.tensor_tensor(mp[:, 0:n, 2], rest_, mp[:, 0:n, 1], ALU.subtract).then_inc(negm, 1)

                def reciprocals(sidx, i):
                    if i == 0:
                        dve.wait_ge(d_ready, sidx + 2)
                        dve.wait_ge(fin_done, sidx + 1)
                    ins = nc.vector.reciprocal(Rr[:, i * QUART:(i + 1) * QUART], PS[:, 7, i * QUART:(i + 1) * QUART])
                    if i == 3:
                        ins.then_inc(recip, 1)

                def superblock(sidx, half, base, first):
                    for j in range(NQ):
                        if half < 2:
                            for i in tiles_at(NQ * half + j):
                                max_tile(i, base, PLAN[i][1])
                            if j == SPLIT_STEP:
                                if half == 0:
                                    split_max(sidx + 1, base + 3 * TILES, 0, 6)
                                else:
                                    split_max(sidx + 1, base + PAIR_TILES, 6, 8)
                        if FINISH_STEP <= j < FINISH_STEP + 4 and not first:
                            reciprocals(sidx - 1, j - FINISH_STEP)
                        if j in DVE_SUMS:
                            r = key_rows(j)
                            dve.wait_ge(exp_done, NQ * sidx + j + 1)
                            e = Pb[0:r, j % PSLOTS, :, :]
                            if j == DVE_SUMS[0]:
                                dve.wait_ge(d_ready, sidx + 1)
                                nc.vector.tensor_copy(accD[0:r, :, :], e).then_inc(psum_dve, 1)
                            else:
                                dve.wait_ge(psum_dve, NDVE * (sidx + 1) + dve_sums_upto(j) - 1)
                                nc.vector.tensor_tensor(accD[0:r, :, :], accD[0:r, :, :], e,
                                                        ALU.add).then_inc(psum_dve, 1)

                for i in range(FIRST_TILES):
                    max_tile(i, GROUP_TILES * g, 4 + i % 2)
                split_max(NJ * g, GROUP_TILES * g + FIRST_TILES, 0, 8)

                def pair_of(t, first):
                    base = GROUP_TILES * g + FIRST_TILES + PAIR_TILES * t
                    superblock(NJ * g + 2 * t, 0, base, first)
                    superblock(NJ * g + 2 * t + 1, 1, base, False)

                pair_of(0, True)
                with dve.Fori(1, NJ // 2) as t:
                    pair_of(t, False)
                superblock(NJ * g + NJ - 1, 2, 0, False)
                for i in range(4):
                    reciprocals(NJ * g + NJ - 1, i)
                assert n[0] == LINKS, n[0]

        @block.scalar
        def _(act):
            act.sem_inc(pv_done, PSLOTS)
            act.wait_ge(borders, 1)
            with act.Fori(0, GROUPS) as g:
                def normalise(layer, dst, src, done):
                    for j in range(NJ):
                        nc.scalar.activation(dst(j), rows(src[:, j * CH:(j + 1) * CH]), ACT.Identity,
                                             bias=nb[:, :], scale=rstd[:, :]).then_inc(done, 1)

                def padded(t):
                    return lambda j: pad_rows(t, ROWS * j + 1, ROWS, 1)

                act.wait_ge(gn_nb[0], g + 1)
                normalise(0, padded(xnp), xin, xn_ready[0])
                for j in range(NJ):
                    act.wait_ge(sft_ready, NJ * g + j + 1)
                    nc.scalar.activation(rows(SF[:, j * CH:(j + 1) * CH]), pad_rows(sTb[0:3 * PITCH, j, :], 0, ROWS),
                                         ACT.Copy).then_inc(SF_ready, 1)
                act.wait_ge(gn_nb[1], g + 1)
                normalise(1, padded(xnp), xw, xn_ready[1])
                act.wait_ge(U_ready, g + 1)
                for j in range(NJ):
                    act.wait_ge(l1_ps, NJ * g + j + 1)
                    if j >= 2:
                        act.wait_ge(gated_ready, NJ * g + j - 1)
                    nc.scalar.activation(att[:, j % 2, :], PS[:, 3 + j % 3, 0:CH], ACT.Sigmoid,
                                         bias=uc[:, 1:2]).then_inc(att_ready, 1)
                act.wait_ge(gn_nb[2], g + 1)
                for j in range(NJ):
                    src = rows(xw[:, j * CH:(j + 1) * CH])
                    nc.scalar.activation(pad_rows(xh, ROWS * j + 1, ROWS, 1), src, ACT.Identity,
                                         bias=nb[:, :], scale=rstd[:, :])
                    nc.scalar.activation(pad_rows(xnp, ROWS * j + 1, ROWS, 1), src, ACT.Identity,
                                         bias=nb[:, :], scale=rstd[:, :]).then_inc(xn_ready[2], 1)
                act.wait_ge(gn_nb[3], g + 1)
                normalise(3, lambda j: rows(xnf[:, j * CH:(j + 1) * CH]), xw, xn_ready[3])

                def middle_part(j):
                    act.wait_ge(rest_h, NJ * g + j + 1)
                    nc.scalar.activation(parts[:, 1, j * CH:(j + 1) * CH], rest[:, j % 2, :],
                                         ACT.Copy).then_inc(part_m, 1)

                for j in range(NJ):
                    act.wait_ge(qk_ps, NJ * g + j + 1)
                    if j == 0:
                        act.wait_ge(qk_loaded, 16 * (24 * g + 1))
                    nc.scalar.activation(parts[:, 0, j * CH:(j + 1) * CH], PS[0:4 * DK, j, 0:CH],
                                         ACT.Copy).then_inc(part_h, 1)
                    if j:
                        middle_part(j - 1)
                middle_part(NJ - 1)
                for i in range(NJ):
                    m = min(4, NQ - 4 * i)
                    r = key_rows(NQ - 1) if m < 4 else QC
                    act.wait_ge(v_ps, NJ * g + i + 1)
                    nc.scalar.activation(VT[0:r, 4 * i:4 * i + m, :],
                                         PS[0:r, i, 0:m * P].rearrange("p (a b) -> p a b", b=P),
                                         ACT.Copy).then_inc(v_ready, 1)

                def max_rows(sidx, col, n):
                    act.wait_ge(mrow_ps, sidx + 1)
                    nc.scalar.activation(Qa[KROWS:KROWS + 3, :, ds(col, n * BLK)],
                                         rowb[KROWS:KROWS + 3, :].rearrange("p (h n) -> p h n", h=2)[:, :, 0:n * BLK],
                                         ACT.Copy).then_inc(mrow, 1)

                def exps(sidx, steps, odd, rows_of=None):
                    for j in steps:
                        r = key_rows(j)
                        act.wait_ge(st_ready, NQ * sidx + j + 1)
                        act.wait_ge(pv_done, NQ * sidx + j + 1)
                        i = (j - PSLOTS) % NQ
                        if i in DVE_SUMS:
                            act.wait_ge(psum_dve, NDVE * (sidx + (j >= PSLOTS)) + dve_sums_upto(i))
                        else:
                            act.wait_ge(psum_pool, POOL_SUMS * (sidx + (j >= PSLOTS)) + pool_sums_upto(i))
                        b = 2 * ((j + odd) % 2)
                        nc.scalar.activation(Pb[0:r, j % PSLOTS, :, :], PS[0:r, b:b + 2, 0:CH],
                                             ACT.Exp).then_inc(exp_done, 1)
                        if j == ROWS_STEP + 2 and rows_of:
                            max_rows(sidx + 1, *rows_of)

                def copy_output(sidx):
                    act.wait_ge(pv_done, NQ * (sidx + 1) + PSLOTS)
                    act.wait_ge(fin_done, sidx + 1)
                    nc.scalar.activation(Osb[:, :], PS[:, OB, 0:CH], ACT.Copy).then_inc(ocopy, 1)

                max_rows(NJ * g, 0, 4)
                exps(NJ * g, range(0, TURN), 0)
                with act.Fori(0, NJ // 2) as t:
                    n = NJ * g + 2 * t
                    exps(n, range(TURN, NQ), 0, (2 * CH * t + 4 * BLK, 3))
                    exps(n + 1, range(0, 1), 1)
                    copy_output(n)
                    exps(n + 1, range(1, NQ), 1, (2 * CH * t + 2 * CH, 4))
                    exps(n + 2, range(0, 1), 0)
                    copy_output(n + 1)
                    exps(n + 2, range(1, TURN), 0)
                exps(NJ * g + NJ - 1, range(TURN, NQ), 0)
                copy_output(NJ * g + NJ - 1)

        @block.gpsimd
        def _(pool):
            pool.sem_inc(psum_pool, POOL_SUMS)
            pool.sem_inc(pooltaps, 1)
            pool.sem_inc(pool_step, 2)
            pool.wait_ge(borders, 1)
            pool.wait_ge(consts, 1)
            STEPS = 2 * NJ
            with pool.Fori(0, GROUPS) as g:
                def power(layer):
                    pool.wait_ge(gn_ve[layer], g + 1)
                    nc.gpsimd.tensor_tensor(rstd[:, :], ve[:, :], mhalf[:, 0:1], ALU.pow).then_inc(gn_rstd[layer], 1)

                power(0)
                pool.wait_ge(yvar_ready, g + 1)
                nc.gpsimd.tensor_tensor(ys[:, 4:5], ys[:, 3:4], phalf[:, 0:1], ALU.pow).then_inc(ysd_ready, 1)
                pool.wait_ge(sfvar_ready, g + 1)
                nc.gpsimd.tensor_tensor(sfs[:, 4, :], sfs[:, 3, :], phalf[0:SP2, 0:2 * NSP],
                                        ALU.pow).then_inc(sfsd_ready, 1)
                with pool.Fori(0, NJ) as j:
                    k = NJ * g + j
                    pool.wait_ge(pooltaps, k + 1)
                    pool.wait_ge(prod_ready, TAPS * k + 2 + TAP_BANKS)
                    nc.gpsimd.tensor_tensor(pu[:, 0, :], prod[:, 0, :], prod[:, 1, :], ALU.add)
                    pool.wait_ge(prod_ready, TAPS * k + 4 + TAP_BANKS)
                    nc.gpsimd.tensor_tensor(pu[:, 1, :], prod[:, 2, :], prod[:, 3, :], ALU.add).then_inc(pool_step, 1)
                    pool.wait_ge(pool_step, 2 * k + 3)
                    nc.gpsimd.tensor_tensor(pu[:, 0, :], pu[:, 0, :], pu[:, 1, :], ALU.add).then_inc(pool_step, 1)
                    pool.wait_ge(pool_step, 2 * k + 4)
                    pool.wait_ge(l0_done, k + 1)
                    nc.gpsimd.tensor_tensor(pu[:, 2, :], pu[:, 0, :], xin[:, ds(j * CH, CH)],
                                            ALU.add).then_inc(pooltaps, 1)
                power(1)
                power(2)
                power(3)

                def finish(sidx, s):
                    pool.wait_ge(ocopy, sidx + 2)
                    pool.wait_ge(recip, sidx + 2)
                    nc.gpsimd.tensor_tensor(fin[:, :], Osb[:, :], Rr[:, :], ALU.mult).then_inc(fin_step, 1)
                    pool.wait_ge(fin_step, sidx + 1)
                    nc.gpsimd.tensor_tensor(xw[:, ds(s * CH, CH)], xw[:, ds(s * CH, CH)], fin[:, :],
                                            ALU.add).then_inc(fin_done, 1)

                def superblock(sidx, s, first):
                    for j in range(1, NQ):
                        if j not in DVE_SUMS:
                            pool.wait_ge(exp_done, NQ * sidx + j + 1)
                            if j == 1:
                                nc.gpsimd.tensor_tensor(accQ[:, :, :], Pb[:, 0, :, :], Pb[:, 1, :, :],
                                                        ALU.add).then_inc(psum_pool, 2)
                                continue
                            if j == TO_ACCP:
                                pool.wait_ge(d_ready, sidx + 1)
                            pool.wait_ge(psum_pool, POOL_SUMS * (sidx + 1) + pool_sums_upto(j) - 1)
                            nc.gpsimd.tensor_tensor((accQ if j < TO_ACCP else accP)[:, :, :],
                                                    (accQ if j <= TO_ACCP else accP)[:, :, :],
                                                    Pb[:, j % PSLOTS, :, :], ALU.add).then_inc(psum_pool, 1)
                        if j == FINISH_STEP + 5 and not first:
                            finish(sidx - 1, s - 1)

                superblock(NJ * g, 0, True)
                with pool.Fori(1, NJ) as s:
                    superblock(NJ * g + s, s, False)
                finish(NJ * g + NJ - 1, NJ - 1)

        @block.tensor
        def _(pe):
            mm = nc.tensor.matmul
            pe.sem_inc(accum_ready, 1)
            pe.sem_inc(l0_done, 1)
            pe.wait_ge(consts, 2)
            pe.wait_ge(w_loaded, LOADED)
            with pe.Fori(0, GROUPS) as g:
                def pair_stats(layer):
                    pe.wait_ge(gn_mean[layer], g + 1)
                    mm(small[:, 0:1], pair, mv[:, 0:1], start=True, stop=True).then_inc(gn_pm[layer], 1)
                    pe.wait_ge(gn_sq[layer], g + 1)
                    mm(small[:, 1:2], pair, sq[:, :], start=True, stop=True).then_inc(gn_pv[layer], 1)

                pair_stats(0)
                pe.wait_ge(pooled_ready, 2 * g + 1)
                mm(small[0:2 * MID, 2:3], wcol("w1"), pooled[:, 0:1], start=True, stop=True).then_inc(mid_ready, 1)
                pe.wait_ge(y1_ready, g + 1)
                for t in range(TAPS):
                    last = mm(small[:, 8 + t:9 + t], wcol("w2")[0:2 * MID, t * P:(t + 1) * P], y1[:, :],
                              start=True, stop=True)
                last.then_inc(y_ready, 1)
                pe.wait_ge(xn_ready[0], NJ * (g + 1))
                pe.wait_ge(ocopy, NJ * g + 1)
                for i in range(NSP):
                    last = mm(PS[0:SP2, OB, i * PART:(i + 1) * PART], xnp[:, (2 * i + 1) * PW + 1:(2 * i + 3) * PW + 1], wcol("ws"),
                              start=True, stop=True)
                last.then_inc(sfT_ready, 1)
                pe.wait_ge(sfp_ready, g + 1)
                for j in range(NJ):
                    for i in range(4):
                        last = nc.tensor.transpose(sTb[0:3 * PITCH, j, i * SP2:(i + 1) * SP2],
                                                   sfp[:, 4 * j + i, :, :].rearrange("p a b -> p (a b)"),
                                                   identb[0:SP2, 0:SP2])
                    last.then_inc(sft_ready, 1)

                def spread_tap(j, t):
                    k = NJ * g + j
                    pe.wait_ge(prod_ready, TAPS * k + t + 1)
                    mm(PS[:, t % TAP_BANKS, 0:CH], selb[:, t, :], SF[:, ds(j * CH, CH)],
                       start=True, stop=True).then_inc(tap_ready, 1)

                def add_tap(j, t):
                    k = NJ * g + j
                    pe.wait_ge(prod_ready, TAPS * k + t + 1 + TAP_BANKS)
                    if t == POOL_TAPS:
                        pe.wait_ge(l0_done, k + 1)
                    ins = mm(PS[:, ACCB, 0:CH], identf, prod[:, t, :], start=(t == POOL_TAPS), stop=(t == TAPS - 1))
                    if t == TAPS - 1:
                        ins.then_inc(accum_ready, 1)

                def taps(j, first):
                    for t in range(TAPS):
                        spread_tap(j, t)
                        if t in (1, 2) and not first:
                            add_tap(j - 1, TAPS - 3 + t)
                        if t - 2 >= POOL_TAPS:
                            add_tap(j, t - 2)

                pe.wait_ge(SF_ready, NJ * (g + 1))
                taps(0, True)
                with pe.Fori(1, NJ) as j:
                    taps(j, False)
                add_tap(NJ - 1, TAPS - 2)
                add_tap(NJ - 1, TAPS - 1)

                pair_stats(1)
                pe.wait_ge(pooled_ready, 2 * g + 2)
                mm(small[0:2 * CR, 20:21], wcol("wk"), pooled[:, 1:2], start=True, stop=True).then_inc(km_ps, 1)
                pe.wait_ge(km_ready, g + 1)
                mm(small[:, 21:22], wcol("wq")[0:2 * CR], km[:, 0:1], start=True, stop=True)
                mm(small[:, 22:23], half8[0:2 * CR], km[:, 1:2], start=True, stop=True).then_inc(u_ps, 1)
                for j in range(NJ):
                    pe.wait_ge(xn_ready[1], NJ * g + j + 1)
                    if j == 0:
                        pe.wait_ge(U_ready, g + 1)
                    if j >= 3:
                        pe.wait_ge(gated_ready, NJ * g + j - 2)
                    xnj = pad_rows(xnp, ROWS * j + 1, ROWS, 1)
                    mm(PS[:, j % 3, 0:CH], wcol("wv"), xnj, start=True, stop=True)
                    mm(PS[:, 3 + j % 3, 0:CH], U[:, :], xnj, start=True, stop=True).then_inc(l1_ps, 1)

                pair_stats(2)
                with pe.Fori(0, NJ) as j:
                    pe.wait_ge(xl_ready, NJ * (g + 1))
                    for src in (xh, xl):
                        for t in range(TAPS):
                            last = mm(PS[:, j, 0:CH], wt[:, t * P:(t + 1) * P],
                                      pad_rows_at(src, j * (ROWS * PW) + (t // 3) * PW + t % 3, ROWS),
                                      start=(src is xh and t == 0), stop=(src is xl and t == TAPS - 1))
                    last.then_inc(conv_ready, 1)

                pair_stats(3)
                for j in range(NJ):
                    pe.wait_ge(xn_ready[3], NJ * g + j + 1)
                    mm(PS[0:4 * DK, j, 0:CH], wcol("qk3"), xnf[:, j * CH:(j + 1) * CH],
                       start=True, stop=True).then_inc(qk_ps, 1)
                for j in range(NQ):
                    r = key_rows(j)
                    if j % 4 == 0:
                        pe.wait_ge(rest_h, NJ * g + j // 4 + 1)
                    last = mm(PS[0:r, j // 4, (j % 4) * P:(j % 4 + 1) * P], xnf[:, j * QC:j * QC + r], wcol("wv3"),
                              start=True, stop=True)
                    if j % 4 == 3 or j == NQ - 1:
                        last.then_inc(v_ps, 1)

                def max_tile(i, base, bank, left, col):
                    blk, h, t = i // TILES, i // NJ % 2, i % NJ
                    pe.wait_ge(mx_free, base + left + 1)
                    mm(PS[0:BLK, bank, 0:CH], Qa[0:KROWS, h, ds(col + blk * BLK, BLK)],
                       Ka[0:KROWS, h, t * CH:(t + 1) * CH], start=True, stop=True).then_inc(mx_ready, 1)

                def max_rows(sidx, n):
                    pe.wait_ge(negm, sidx + 1)
                    for i in range(2 * n):
                        at = (i % 2) * 4 * BLK + (i // 2) * BLK
                        last = nc.tensor.transpose(rowb[KROWS:KROWS + 3, at:at + BLK], mp[:, i, :], identb[:, :])
                    last.then_inc(mrow_ps, 1)

                def scores(k, s, h):
                    j = k % NQ
                    r = key_rows(j)
                    ins = mm(PS[0:r, 2 * (k % 2) + h, 0:CH], Ka[0:KROWS + 3, h, j * QC:j * QC + r],
                             Qa[0:KROWS + 3, h, ds(s * CH, CH)], start=True, stop=True)
                    if h == 1:
                        ins.then_inc(st_ready, 1)

                def denominators(sidx):
                    pe.wait_ge(psum_pool, POOL_SUMS * (sidx + 2))
                    pe.wait_ge(psum_dve, NDVE * (sidx + 2))
                    for h in range(2):
                        mm(PS[C * h:C * h + C, 7, 0:CH], ones[:, :], accP[:, h, :], start=True, stop=False)
                        last = mm(PS[C * h:C * h + C, 7, 0:CH], ones[:, :], accD[:, h, :], start=False, stop=True)
                    last.then_inc(d_ready, 1)

                def superblock(s, half, base, col, first):
                    sidx = NJ * g + s
                    seen7 = False
                    for j in range(NQ):
                        k = NQ * (half % 2) + j
                        tiles = [] if half == 2 else tiles_at(k)

                        def next_tile(seen7):
                            if tiles:
                                i = tiles.pop(0)
                                if PLAN[i][1] == 7 and not seen7:
                                    pe.wait_ge(recip, sidx + 1)
                                    seen7 = True
                                max_tile(i, base, PLAN[i][1], PLAN[i][2], col)
                            return seen7
                        pe.wait_ge(exp_done, NQ * sidx + j + 1)
                        if j == 0:
                            pe.wait_ge(ocopy, sidx + 1)
                        for h in range(2):
                            last = mm(PS[C * h:C * h + C, OB, 0:CH], VT[:, j, C * h:C * h + C],
                                      Pb[:, j % PSLOTS, h, :], start=(j == 0), stop=(j == NQ - 1))
                        last.then_inc(pv_done, 1)
                        for h in range(2):
                            if j < NQ - 2 or half < 2:
                                if j == NQ - 2 and h == 0:
                                    pe.wait_ge(mrow, sidx + 2)
                                scores(k + 2, s + (j >= NQ - 2), h)
                            seen7 = next_tile(seen7)
                        while tiles:
                            seen7 = next_tile(seen7)
                        if j == FINISH_STEP - 1 and not first:
                            denominators(sidx - 1)
                        if j == ROWS_STEP and half < 2:
                            max_rows(sidx + 1, 3 + half)

                def pair_of(t, first):
                    base = GROUP_TILES * g + FIRST_TILES + PAIR_TILES * t
                    col = 2 * CH * t + 4 * BLK
                    superblock(2 * t, 0, base, col, first)
                    superblock(2 * t + 1, 1, base, col, False)

                pe.wait_ge(v_ready, NJ * (g + 1))
                pe.wait_ge(qk_loaded, 16 * (24 * (g + 1) + 1))
                for i in range(FIRST_TILES):
                    max_tile(i, GROUP_TILES * g, 4 + i % 2, max(i - 1, 0), 0)
                max_rows(NJ * g, 4)
                pe.wait_ge(mrow, NJ * g + 1)
                for j in range(2):
                    for h in range(2):
                        scores(j, 0, h)
                pair_of(0, True)
                with pe.Fori(1, NJ // 2) as t:
                    pair_of(t, False)
                superblock(NJ - 1, 2, 0, 0, False)
                denominators(NJ * g + NJ - 1)


def constants(np):
    c = np.zeros((P, CCOLS), np.float32)
    p = np.arange(P)
    c[:, 0:P] = np.eye(P)
    c[:, P:2 * P] = 0.5 * (p[:, None] // 2 == p[None, :] // 2)
    c[:, 2 * P:3 * P] = p[:, None] // C == p[None, :] // C
    c[0:2 * CR, 3 * P:4 * P] = p[0:2 * CR, None] // CR == p[None, :] // C
    for part in range(3):
        for h in range(2):
            for t in range(TAPS):
                a = 4 * P + t * P + C * h
                c[part * PITCH + h * TAPS + t, a:a + C] = 1.0
    return c


def kernel(**inputs):
    import numpy as np
    import concourse.bacc as bacc
    from concourse.bass_utils import run_bass_kernel_spmd

    a = {k: np.asarray(w) for k, w in inputs.items()}
    arrays = {
        "x": a["x"].reshape(GROUPS, P, HW),
        "w1t": a["L0_conv_w1"].T, "b1": a["L0_conv_b1"].reshape(MID, 1),
        "w2t": a["L0_conv_w2"].reshape(C, TAPS, MID).transpose(2, 1, 0),
        "b2": a["L0_conv_b2"].reshape(C, TAPS),
        "wst": a["L0_conv_ws"].T, "bs": a["L0_conv_bs"], "fn": a["L0_conv_fn_std"].reshape(C, TAPS),
        "wq": a["L1_conv_Wq"], "bq": a["L1_conv_bq"].reshape(CR, 1),
        "wkt": a["L1_conv_Wk"].T, "bk": a["L1_conv_bk"].reshape(CR, 1),
        "wvt": a["L1_conv_Wv"].T, "bv": a["L1_conv_bv"].reshape(C, 1),
        "wc": a["L2_conv_weight"].transpose(1, 2, 3, 0).reshape(C, TAPS, C),
        "bc": a["L2_conv_bias"].reshape(C, 1),
        "q3t": a["L3_conv_q_w"].T, "k3t": a["L3_conv_k_w"].T, "v3t": a["L3_conv_v_w"].T,
        "cst": constants(np),
    }
    nc = bacc.Bacc("TRN2", target_bir_lowering=False, num_devices=1)
    arrays = {f"in_{k}": np.ascontiguousarray(w) for k, w in arrays.items()}
    args = [nc.dram_tensor(k, w.shape, mybir.dt.from_np(w.dtype), kind="ExternalInput").ap()
            for k, w in arrays.items()]
    out = nc.dram_tensor("out", (GROUPS, P, HW), F32, kind="ExternalOutput").ap()
    build(nc, *args, out)
    r = run_bass_kernel_spmd(nc, [arrays], core_ids=[0])
    return r.results[0]["out"].reshape(B, C, H, W)
```

```python
from contextlib import ExitStack

import concourse.bass as bass
from concourse import mybir

F32 = mybir.dt.float32
F32R = mybir.dt.float32r
BF16 = mybir.dt.bfloat16
ALU = mybir.AluOpType
ACT = mybir.ActivationFunctionType
X = mybir.AxisListType.X
ds = bass.ds

B, C, H, W = 8, 64, 56, 56
P = 2 * C
GROUPS = B // 2
HW = H * W
ROWS = 8
CH = ROWS * W
NJ = HW // CH
PW = W + 2
PADDED = PW * (H + 2) + 4
TAPS = 9
MID = 12
CR = 8
DK = 16
GAIN_OVER_K = float(2.0 ** 0.5) / 3
THRESHOLD = 0.05
SP2 = 2 * PW
NSP = H // 2
PART = 2 * TAPS
SPREADS = 12
PITCH = 32
QC = 128
NQ = -(-HW // QC)
KROWS = 6 * DK
QUART = CH // 4
BLK = 128
HWQ = -(-HW // BLK) * BLK
EARLY_TILES = 2
FINISH_STEP = 3
TILES = 2 * NJ
PAIR_TILES = 7 * TILES
GROUP_TILES = (NJ // 2) * PAIR_TILES
FIRST_TILES = 4 * TILES
PSLOTS = 5
TAP_BANKS = 3
PE_TAPS = TAPS // 2 + 1
POOL_STEPS = 3
DVE_SUMS = (3, 7, 11, 15, 19, 23, 24)
TURN = 7
FRONT_XN = 7
FRONT_SF = 8
FRONT_TR = (20, 20, 21, 22, 23, 24, 24)
FRONT_ROOT = 16
TO_ACCP = 5
SPLIT_STEP = 19
ROWS_STEP = 21
FREE7 = range(8, SPLIT_STEP)


DENSITY = [2] * 3 + [1.5] * 5 + [2.4] * 12 + [1.6, 0.3, 1.6, 2.2, 2.2]


def plan_tiles():
    plan, steps, held = [], [], {4: 0, 5: 0, 7: 0}
    early = 3 * TILES
    for span, tiles in ((range(0, SPLIT_STEP + 1), early),
                        (range(SPLIT_STEP + 1, NQ + SPLIT_STEP + 1), PAIR_TILES - early)):
        total = sum(DENSITY[i % NQ] for i in span)
        done = 0
        for i in span:
            steps += [i] * (round(tiles * (done + DENSITY[i % NQ]) / total) - round(tiles * done / total))
            done += DENSITY[i % NQ]
    for i, step in enumerate(steps):
        banks = (4, 5, 7) if step % NQ in FREE7 else (4, 5)
        bank = min(banks, key=lambda b: held[b])
        plan.append((step, bank, held[bank]))
        held[bank] = i + 1
    return plan


PLAN = plan_tiles()

COLS = {}
_at = 0
for _name, _n in (("w1", 2 * MID), ("ws", PART), ("wv", P), ("wk", 2 * CR), ("qk3", 4 * DK), ("wv3", P),
                  ("w2", TAPS * P), ("wq", P), ("conv", TAPS * P)):
    COLS[_name] = (_at, _at + _n)
    _at += _n
WCOLS = _at
VEC = {"b2": (0, 9), "fn": (9, 18), "b1": (18, 19), "bk": (19, 20), "bq": (20, 21), "bv": (21, 22),
       "bc": (22, 23), "bs": (23, 32)}
VCOLS = 32
CST = {"ident": (0, P), "pair": (P, 2 * P), "half": (2 * P, 3 * P), "half8": (3 * P, 4 * P),
       "sel": (4 * P, (4 + TAPS) * P)}
CCOLS = (4 + TAPS) * P


def key_rows(j):
    return min(QC, HW - j * QC)


def pool_sums_upto(j):
    return sum(1 for i in range(max(j, 1) + 1) if i not in DVE_SUMS)


def dve_sums_upto(j):
    return sum(1 for i in range(j + 1) if i in DVE_SUMS)


POOL_SUMS = pool_sums_upto(NQ - 1)
NDVE = len(DVE_SUMS)


def tiles_at(step):
    return [i for i, (at, _, _) in enumerate(PLAN) if at == step]


def build(nc, x, weights, vectors, cst, out):
    with ExitStack() as ctx:
        def sb(name, shape, dt=F32):
            return ctx.enter_context(nc.sbuf_tensor(name, shape, dt))

        def sem(name):
            return ctx.enter_context(nc.semaphore(name))

        xin = sb("xin", [P, HW])
        xw = sb("xw", [P, HW])
        xnp = sb("xnp", [P, PADDED])
        xh = sb("xh", [P, PADDED], F32R)
        xl = sb("xl", [P, PADDED], F32R)
        xnf = sb("xnf", [P, HW])
        wz = sb("wz", [P, WCOLS])
        wt = sb("wt", [P, TAPS * P], F32R)
        vec = sb("vec", [P, VCOLS])
        cs = sb("cs", [P, CCOLS])
        selb = sb("selb", [3 * PITCH, TAPS, P], BF16)
        identb = sb("identb", [P, P], BF16)
        ones = sb("ones", [P, C])
        mhalf = sb("mhalf", [P, 1])
        phalf = sb("phalf", [P, 1])
        st6 = sb("st6", [P, NJ, 6])
        mv = sb("mv", [P, 2])
        idle = sb("idle", [P, 1])
        junk = sb("junk", [P, 1])
        dm = sb("dm", [P, 1])
        sq = sb("sq", [P, 1])
        ve = sb("ve", [P, 1])
        rstd = sb("rstd", [P, 1])
        nb = sb("nb", [P, 1])
        pooled = sb("pooled", [P, 2])
        y1 = sb("y1", [2 * MID, 1])
        yf = sb("yf", [P, TAPS])
        ysq = sb("ysq", [P, TAPS])
        ys = sb("ys", [P, 6])
        cf = sb("cf", [P, TAPS])
        sf = sb("sf", [SP2, NSP * 2, TAPS])
        sf2 = sb("sf2", [SP2, NSP * 2, TAPS])
        sfs = sb("sfs", [SP2, 6, NSP * 2])
        wsm = sb("wsm", [P, 3])
        sfp = sb("sfp", [SP2, NSP, 3, PITCH], BF16)
        km = sb("km", [2 * CR, 2])
        uc = sb("uc", [P, 2])
        U = sb("U", [P, P])
        parts = sb("parts", [4 * DK, 3, HW], BF16)
        Qa = sb("Qa", [P, 2, HWQ], BF16)
        Ka = sb("Ka", [P, 2, HW], BF16)
        VT = sb("VT", [QC, NQ, P])
        Pb = sb("Pb", [QC, PSLOTS, 2, CH])
        flat = Pb[:, :, :, :].rearrange("p a b c -> p (a b c)")
        tneg = flat[:, 0:TAPS * P]
        prod = flat[:, 0:TAPS * CH].rearrange("p (t n) -> p t n", t=TAPS)
        rest = flat[0:4 * DK, 0:HW].rearrange("p (a n) -> p a n", a=NJ)
        flat = VT[:, :, :].rearrange("p a b -> p (a b)")
        pu = flat[:, 0:3 * CH].rearrange("p (a n) -> p a n", a=3)
        SF = xnf[0:3 * PITCH, 0:HW // 2].bitcast(BF16)
        accP = sb("accP", [QC, 2, CH])
        accQ = sb("accQ", [QC, 2, CH])
        accD = sb("accD", [QC, 2, CH])
        att, gated = accP, accD
        nmt = sb("nmt", [BLK, PAIR_TILES // NJ, NJ])
        nm = sb("nm", [BLK, 2, 8])
        mp = sb("mp", [BLK, 8, 3], BF16)
        Osb = sb("Osb", [P, CH])
        Rr = sb("Rr", [P, CH])
        fin = sb("fin", [P, CH])

        PS = ctx.enter_context(nc.psum_tensor("PS", [P, 8, 512], F32))
        small = PS[:, 7, :]
        ACCB = 4
        OB = 6
        FB = 4
        SFB = 5
        front = PS[:, FB, :]
        sTb = PS[:, FB:SFB + 1, :].bitcast(BF16)
        rowb = PS[:, 7, :].bitcast(BF16)

        def pad_rows(t, r0, n, c0=0):
            return t[:, r0 * PW + c0:(r0 + n) * PW + c0].rearrange("p (r w) -> p r w", w=PW)[:, :, 0:W]

        def pad_rows_at(t, off, n):
            return t[:, ds(off, n * PW)].rearrange("p (r w) -> p r w", w=PW)[:, :, 0:W]

        def rows(ap):
            return ap.rearrange("p (r w) -> p r w", w=W)

        def wcol(name):
            return wz[:, COLS[name][0]:COLS[name][1]]

        def v(name, n=P):
            return vec[0:n, VEC[name][0]:VEC[name][1]]

        identf = cs[:, CST["ident"][0]:CST["ident"][1]]
        pair = cs[:, CST["pair"][0]:CST["pair"][1]]
        halfm = cs[:, CST["half"][0]:CST["half"][1]]
        half8 = cs[:, CST["half8"][0]:CST["half8"][1]]

        w_loaded = sem("weights_loaded")
        taps_loaded = sem("tap_weights_loaded")
        borders = sem("borders_zeroed")
        consts = sem("constants_ready")
        ternary = sem("ternary_weights_ready")
        setup = sem("vector_set_up")
        cleared = sem("memory_cleared")
        x_loaded = sem("x_loaded")
        dve_step = sem("dve_step")
        gn_mean = [sem(f"gn_mean_{i}") for i in range(4)]
        gn_pm = [sem(f"gn_pair_mean_{i}") for i in range(4)]
        gn_sq = [sem(f"gn_squares_{i}") for i in range(4)]
        gn_pv = [sem(f"gn_pair_var_{i}") for i in range(4)]
        gn_ve = [sem(f"gn_var_eps_{i}") for i in range(4)]
        gn_rstd = [sem(f"gn_rstd_{i}") for i in range(4)]
        gn_nb = [sem(f"gn_bias_{i}") for i in range(4)]
        pooled_ready = sem("pooled_ready")
        xn_ready = [sem(f"xn_ready_{i}") for i in range(4)]
        mid_ready = sem("mid_ready")
        y1_ready = sem("y1_ready")
        y_ready = sem("y_ready")
        yvar_ready = sem("yvar_ready")
        ysd_ready = sem("ysd_ready")
        sfT_ready = sem("sfT_ready")
        sfvar_ready = sem("sfvar_ready")
        sfsd_ready = sem("sfsd_ready")
        sfp_ready = sem("sf_parts_ready")
        sft_ready = sem("sf_transposed")
        SF_ready = sem("SF_ready")
        tap_ready = sem("tap_ready")
        prod_ready = sem("prod_ready")
        tap_added = sem("tap_added")
        pool_step = sem("pool_step")
        pooltaps = sem("pool_taps_summed")
        l0_done = sem("l0_chunk_done")
        km_ps = sem("km_in_psum")
        km_ready = sem("km_ready")
        u_ps = sem("u_in_psum")
        U_ready = sem("U_ready")
        l1_ps = sem("l1_in_psum")
        att_ready = sem("att_ready")
        gated_ready = sem("gated_ready")
        l1_done = sem("l1_chunk_done")
        xh_ready = sem("xh_ready")
        xl_ready = sem("xl_ready")
        conv_ready = sem("conv_ready")
        l2_done = sem("l2_chunk_done")
        qk_ps = sem("qk_in_psum")
        part_h = sem("qk_part_high")
        rest_h = sem("qk_rest")
        part_m = sem("qk_part_middle")
        part_l = sem("qk_part_low")
        qk_loaded = [sem(f"qk_rows_loaded_{h}") for h in range(2)]
        first_ready = sem("first_max_scores_ready")
        first_used = sem("first_max_scores_reduced")
        v_ps = sem("v_in_psum")
        v_ready = sem("v_ready")
        mx_ready = sem("max_scores_ready")
        mx_free = sem("max_bank_free")
        mxstep = sem("max_split_step")
        negm = sem("negmax_parts_ready")
        mrow_ps = sem("max_rows_in_psum")
        mrow = sem("max_rows_ready")
        st_ready = sem("scores_ready")
        exp_done = sem("exp_done")
        pv_done = sem("pv_done")
        psum_pool = sem("exps_summed_by_pool")
        psum_dve = sem("exps_summed_by_dve")
        ocopy = sem("output_copied")
        d_ready = sem("denominators_ready")
        recip = sem("reciprocals_ready")
        fin_step = sem("normalised")
        fin_done = sem("l3_chunk_done")
        stored = sem("stored")

        FRONT_LINKS, LINKS = 23, 31

        block = ctx.enter_context(nc.Block())

        @block.sync
        def _(sp):
            sp.dma_start(xin[:, :], x[0]).then_inc(x_loaded, 16)
            few, sel = COLS["conv"][0], CST["sel"][0]
            for dst, src in ((cs[:, 0:sel], cst[:, 0:sel]), (vec[:, :], vectors), (wz[:, 0:few], weights[:, 0:few])):
                sp.dma_start(dst, src).then_inc(w_loaded, 16)
            for dst, src in ((cs[:, sel:], cst[:, sel:]), (wz[:, few:], weights[:, few:])):
                sp.dma_start(dst, src).then_inc(taps_loaded, 16)
            sp.sem_inc(stored, 16)
            for loaded in qk_loaded:
                sp.sem_inc(loaded, 16)
            for first in (ocopy, d_ready, recip, fin_done):
                sp.sem_inc(first, 1)

            def spread(part, h):
                for dst, base, order in ((Qa, 2 * DK * h, (0, 0, 1, 0, 2, 1)),
                                         (Ka, 2 * DK * h + DK, (0, 1, 0, 2, 0, 1))):
                    for r in range(KROWS // DK):
                        if order[r] == part:
                            sp.dma_start(dst[DK * r:DK * r + DK, h, 0:HW],
                                         parts[base:base + DK, part, :]).then_inc(qk_loaded[h], 16)

            def store(g):
                with sp.Fori(0, NJ) as s:
                    sp.wait_ge(fin_done, NJ * g + s + 2)
                    sp.dma_start(out[g][:, ds(s * CH, CH)], xw[:, ds(s * CH, CH)]).then_inc(stored, 16)

            def group(g, last):
                for h in range(2):
                    for part, ready in enumerate((part_h, part_m, part_l)):
                        if h == 0:
                            sp.wait_ge(ready, NJ * g + NJ)
                        spread(part, h)
                if not last:
                    sp.dma_start(xin[:, :], x[g + 1]).then_inc(x_loaded, 16)
                store(g)

            with sp.Fori(0, GROUPS - 1) as g:
                group(g, False)
            group(GROUPS - 1, True)
            sp.wait_ge(stored, 16 * (NJ * GROUPS + 1))

        def low_part(dve, g, j):
            c = slice(j * CH, (j + 1) * CH)
            dve.wait_ge(part_m, NJ * g + j + 1)
            nc.vector.tensor_tensor(parts[:, 2, c], rest[:, j, :], parts[:, 1, c],
                                    ALU.subtract).then_inc(part_l, 1)

        @block.vector
        def _(dve):
            nc.vector.memset(xnp[:, :], 0.0).then_inc(borders, 1)
            nc.vector.memset(mhalf[:, :], -0.5)
            nc.vector.memset(phalf[:, :], 0.5)
            nc.vector.memset(ones[:, :], 1.0)
            nc.vector.memset(sfp[:, :, :, :], 0.0).then_inc(setup, 1)
            dve.sem_inc(prod_ready, TAP_BANKS)
            dve.sem_inc(mx_free, 1)
            dve.sem_inc(first_used, NJ)
            dve.sem_inc(psum_dve, NDVE)

            def centre_weights():
                wsv = wcol("ws").rearrange("p (h t) -> p h t", h=2)
                dve.wait_ge(w_loaded, 3 * 16)
                nc.vector.reduce_sum(wsm[:, 0:2], wsv, X)
                nc.vector.reduce_sum(wsm[:, 2:3], v("bs"), X).then_inc(consts, 1)
                dve.wait_ge(consts, 1)
                nc.vector.scalar_tensor_tensor(out=wsv, in0=wsm[:, 0:2].unsqueeze(2).to_broadcast([P, 2, TAPS]),
                                               scalar=-1.0 / TAPS, in1=wsv, op0=ALU.mult, op1=ALU.add)
                nc.vector.scalar_tensor_tensor(out=v("bs"), in0=wsm[:, 2:3].to_broadcast([P, TAPS]),
                                               scalar=-1.0 / TAPS, in1=v("bs"), op0=ALU.mult,
                                               op1=ALU.add).then_inc(consts, 1)

            def tap_constants():
                dve.wait_ge(taps_loaded, 2 * 16)
                nc.vector.tensor_copy(selb[:, :, :], cs[0:3 * PITCH, CST["sel"][0]:CST["sel"][1]]
                                      .rearrange("p (t c) -> p t c", t=TAPS))
                nc.vector.tensor_copy(identb[:, :], identf)
                nc.vector.tensor_scalar(tneg, wcol("conv"), -THRESHOLD, None, ALU.is_lt)
                nc.vector.tensor_scalar(wcol("conv"), wcol("conv"), THRESHOLD, None, ALU.is_gt).then_inc(ternary, 1)
                dve.wait_ge(ternary, 1)
                nc.vector.tensor_tensor(wt[:, :], wcol("conv"), tneg, ALU.subtract).then_inc(ternary, 1)

            n = [0]

            def link(g, ins):
                n[0] += 1
                ins.then_inc(dve_step, 1)
                dve.wait_ge(dve_step, LINKS * g + n[0])

            def chunk_stats(src, j):
                return nc.vector.bn_stats(st6[:, j, :], src[:, j * CH:(j + 1) * CH])

            def mean_var(g, layer, last):
                link(g, last)
                nc.vector.memset(idle[:, :], 0.0)
                nc.vector.bn_aggr(mv[:, :], st6[:, :, :].rearrange("p a b -> p (a b)")).then_inc(gn_mean[layer], 1)

            def squares(g, layer, bank):
                dve.wait_ge(gn_pm[layer], g + 1)
                link(g, nc.vector.tensor_tensor(dm[:, :], mv[:, 0:1], bank[:, 0:1], ALU.subtract))
                nc.vector.scalar_tensor_tensor(out=sq[:, :], in0=dm[:, :], scalar=dm[:, :], in1=mv[:, 1:2],
                                               op0=ALU.mult, op1=ALU.add).then_inc(gn_sq[layer], 1)

            def var_eps(g, layer, bank):
                dve.wait_ge(gn_pv[layer], g + 1)
                nc.vector.tensor_scalar(ve[:, :], bank[:, 1:2], 1e-5, None, ALU.add).then_inc(gn_ve[layer], 1)

            def bias(g, layer, bank):
                dve.wait_ge(gn_rstd[layer], g + 1)
                nc.vector.scalar_tensor_tensor(out=nb[:, :], in0=bank[:, 0:1], scalar=-1.0, in1=rstd[:, :],
                                               op0=ALU.mult, op1=ALU.mult).then_inc(gn_nb[layer], 1)

            def stats(g, layer, last):
                mean_var(g, layer, last)
                squares(g, layer, small)
                var_eps(g, layer, small)
                bias(g, layer, small)

            def front_stats(g):
                n[0] = 0
                dve.wait_ge(x_loaded, 16 * g + 16)
                for i in range(NJ - 1):
                    chunk_stats(xin, i)
                mean_var(g, 0, chunk_stats(xin, NJ - 1))

            def front_bias(g):
                bias(g, 0, front)
                nc.vector.tensor_tensor(pooled[:, 0:1], dm[:, :], rstd[:, :], ALU.mult).then_inc(pooled_ready, 1)

            def front_mid(g):
                dve.wait_ge(mid_ready, g + 1)
                nc.vector.tensor_scalar(y1[:, :], front[0:2 * MID, 2:3], v("b1", 2 * MID), 0.0,
                                        ALU.add, ALU.max).then_inc(y1_ready, 1)

            def front_centre(g):
                dve.wait_ge(y_ready, g + 1)
                link(g, nc.vector.tensor_tensor(yf[:, :], small[:, 8:8 + TAPS], v("b2"), ALU.add))
                link(g, nc.vector.reduce_sum(ys[:, 0:1], yf[:, :], X))
                link(g, nc.vector.tensor_scalar(ys[:, 1:2], ys[:, 0:1], 1.0 / TAPS, None, ALU.mult))
                link(g, nc.vector.tensor_scalar(yf[:, :], yf[:, :], ys[:, 1:2], None, ALU.subtract))
                link(g, nc.vector.tensor_tensor(ysq[:, :], yf[:, :], yf[:, :], ALU.mult))
                link(g, nc.vector.reduce_sum(ys[:, 2:3], ysq[:, :], X))
                nc.vector.tensor_scalar(ys[:, 3:4], ys[:, 2:3], 1.0 / (TAPS - 1), None,
                                        ALU.mult).then_inc(yvar_ready, 1)

            def front_channel_filter(g):
                dve.wait_ge(ysd_ready, g + 1)
                link(g, nc.vector.tensor_scalar(ys[:, 5:6], ys[:, 4:5], 1e-10, None, ALU.add))
                link(g, nc.vector.reciprocal(ys[:, 0:1], ys[:, 5:6]))
                link(g, nc.vector.scalar_tensor_tensor(out=cf[:, :], in0=yf[:, :], scalar=ys[:, 0:1], in1=v("fn"),
                                                       op0=ALU.mult, op1=ALU.mult))
                assert n[0] == FRONT_LINKS, n[0]

            def per_pixel(i):
                return sfs[:, i, :].unsqueeze(2).to_broadcast([SP2, 2 * NSP, TAPS])

            def front_sum_squares(g):
                dve.wait_ge(sfT_ready, g + 1)
                link(g, nc.vector.tensor_tensor(
                    sf[:, :, :], PS[0:SP2, SFB, 0:2 * NSP * TAPS].rearrange("p (n t) -> p n t", t=TAPS),
                    v("bs", SP2).unsqueeze(1).to_broadcast([SP2, 2 * NSP, TAPS]), ALU.add))
                link(g, nc.vector.tensor_tensor(sf2[:, :, :], sf[:, :, :], sf[:, :, :], ALU.mult))
                nc.vector.reduce_sum(sfs[:, 2, :], sf2[:, :, :], X).then_inc(sfvar_ready, 1)

            def front_parts(g):
                dve.wait_ge(sfsd_ready, g + 1)
                link(g, nc.vector.tensor_scalar(sfs[:, 0, :], sfs[:, 4, :], 1e-30, None, ALU.add))
                link(g, nc.vector.reciprocal(sfs[:, 1, :], sfs[:, 0, :]))
                link(g, nc.vector.scalar_tensor_tensor(out=sfs[:, 3, :], in0=sfs[:, 2, :], scalar=0.5 / (TAPS - 1),
                                                       in1=sfs[:, 1, :], op0=ALU.mult, op1=ALU.mult))
                link(g, nc.vector.scalar_tensor_tensor(out=sfs[:, 5, :], in0=sfs[:, 4, :], scalar=0.5,
                                                       in1=sfs[:, 3, :], op0=ALU.mult, op1=ALU.add))
                link(g, nc.vector.tensor_scalar(sfs[:, 0, :], sfs[:, 5, :], 1e-10, None, ALU.add))
                link(g, nc.vector.reciprocal(sfs[:, 3, :], sfs[:, 0, :]))
                link(g, nc.vector.scalar_tensor_tensor(out=sf[:, :, :], in0=sf[:, :, :], scalar=GAIN_OVER_K,
                                                       in1=per_pixel(3), op0=ALU.mult, op1=ALU.mult))
                sfv = sf[:, :, :].rearrange("p (n b) t -> p n (b t)", b=2)
                sf2v = sf2[:, :, :].rearrange("p (n b) t -> p n (b t)", b=2)
                link(g, nc.vector.tensor_copy(sfp[:, :, 0, 0:PART], sfv))
                link(g, nc.vector.tensor_tensor(sf2v, sfv, sfp[:, :, 0, 0:PART], ALU.subtract))
                link(g, nc.vector.tensor_copy(sfp[:, :, 1, 0:PART], sf2v))
                nc.vector.tensor_tensor(sfp[:, :, 2, 0:PART], sf2v, sfp[:, :, 1, 0:PART],
                                        ALU.subtract).then_inc(sfp_ready, 1)

            def group(g, more):
                n[0] = FRONT_LINKS

                def tap(j, t):
                    k = NJ * g + j
                    dve.wait_ge(tap_ready, TAPS * k + t + 1)
                    if t % 2 == 0:
                        dve.wait_ge(tap_added, PE_TAPS * k + t // 2 + 1)
                    elif t < 7:
                        dve.wait_ge(pool_step, POOL_STEPS * k + (1 if t < 5 else 3))
                    else:
                        dve.wait_ge(pooltaps, k + 1)
                    nc.vector.scalar_tensor_tensor(
                        out=rows(prod[:, t, :]), in0=rows(PS[:, t % TAP_BANKS, 0:CH]), scalar=cf[:, t:t + 1],
                        in1=pad_rows_at(xnp, j * (ROWS * PW) + (t // 3) * PW + t % 3, ROWS),
                        op0=ALU.mult, op1=ALU.mult).then_inc(prod_ready, 1)

                def l0_sum(j, odd):
                    dve.wait_ge(tap_added, PE_TAPS * (NJ * g + j + 2))
                    dve.wait_ge(pooltaps, NJ * g + j + 2)
                    dve.wait_ge(stored, 16 * (NJ * g + 1))
                    nc.vector.tensor_tensor(xw[:, ds(j * CH, CH)], PS[:, ACCB + odd, 0:CH], pu[:, 2, :],
                                            ALU.add).then_inc(l0_done, 1)

                for t in range(TAPS):
                    tap(0, t)
                with dve.Fori(0, NJ // 2) as i:
                    for odd in (1, 0):
                        j = 2 * i + 2 - odd
                        for t in range(TAPS):
                            if t == 4:
                                l0_sum(j - 1, 1 - odd)
                            tap(j, t)
                dve.wait_ge(l0_done, NJ * (g + 1) + 1)
                for i in range(NJ - 2):
                    chunk_stats(xw, i)
                l0_sum(NJ - 1, 0)
                chunk_stats(xw, NJ - 2)

                dve.wait_ge(l0_done, NJ * g + NJ + 2)
                stats(g, 1, chunk_stats(xw, NJ - 1))
                nc.vector.tensor_tensor(pooled[:, 1:2], dm[:, :], rstd[:, :], ALU.mult).then_inc(pooled_ready, 1)
                dve.wait_ge(km_ps, g + 1)
                link(g, nc.vector.tensor_tensor(km[:, 0:1], small[0:2 * CR, 20:21], v("bk", 2 * CR), ALU.add))
                nc.vector.tensor_tensor(km[:, 1:2], km[:, 0:1], v("bq", 2 * CR), ALU.mult).then_inc(km_ready, 1)
                dve.wait_ge(u_ps, g + 1)
                link(g, nc.vector.tensor_copy(uc[:, :], small[:, 21:23]))
                nc.vector.tensor_scalar(U[:, :], halfm, uc[:, 0:1], None, ALU.mult).then_inc(U_ready, 1)

                def l1_stats(j):
                    dve.wait_ge(l1_done, NJ * g + j + 1)
                    return chunk_stats(xw, j)

                for j in range(NJ):
                    dve.wait_ge(att_ready, NJ * g + j + 1)
                    if j >= 2:
                        dve.wait_ge(l1_done, NJ * g + j - 1)
                    nc.vector.scalar_tensor_tensor(out=gated[:, j % 2, :], in0=PS[:, j % 3, 0:CH], scalar=v("bv"),
                                                   in1=att[:, j % 2, :], op0=ALU.add,
                                                   op1=ALU.mult).then_inc(gated_ready, 1)
                    if j >= 2:
                        l1_stats(j - 2)
                l1_stats(NJ - 2)

                stats(g, 2, l1_stats(NJ - 1))
                for j in range(NJ):
                    dve.wait_ge(xn_ready[2], NJ * g + j + 1)
                    nc.vector.tensor_tensor(pad_rows(xl, ROWS * j + 1, ROWS, 1), pad_rows(xnp, ROWS * j + 1, ROWS, 1),
                                            pad_rows(xh, ROWS * j + 1, ROWS, 1).bitcast(F32),
                                            ALU.subtract).then_inc(xl_ready, 1)
                for j in range(NJ):
                    c = slice(j * CH, (j + 1) * CH)
                    dve.wait_ge(conv_ready, NJ * g + j + 1)
                    nc.vector.scalar_tensor_tensor(out=xw[:, c], in0=PS[:, j, 0:CH], scalar=v("bc"), in1=xw[:, c],
                                                   op0=ALU.add, op1=ALU.add).then_inc(l2_done, 1)
                    if j:
                        dve.wait_ge(l2_done, NJ * g + j)
                        chunk_stats(xw, j - 1)

                dve.wait_ge(l2_done, NJ * g + NJ)
                stats(g, 3, chunk_stats(xw, NJ - 1))
                for j in range(NJ):
                    c = slice(j * CH, (j + 1) * CH)
                    dve.wait_ge(part_h, NJ * g + j + 1)
                    nc.vector.tensor_tensor(rest[:, j, :], PS[0:4 * DK, j, 0:CH], parts[:, 0, c],
                                            ALU.subtract).then_inc(rest_h, 1)
                for j in range(NJ):
                    low_part(dve, g, j)

                def max_tile(i, base, bank):
                    dve.wait_ge(mx_ready, base + i + 1)
                    nc.vector.reduce_max(nmt[:, i // NJ, i % NJ:i % NJ + 1], PS[0:BLK, bank, 0:CH], X,
                                         negate=True).then_inc(mx_free, 1)

                def first_tile(i):
                    h, blk, t = i // (FIRST_TILES // 2), i // NJ % 4, i % NJ
                    dve.wait_ge(first_ready, FIRST_TILES * g + i + 1)
                    nc.vector.reduce_max(nmt[:, 2 * blk + h, t:t + 1], PS[0:BLK, t, 0:CH], X,
                                         negate=True).then_inc(first_used, 1)

                def split_max(sidx, a, n):
                    def step(ins, k):
                        ins.then_inc(mxstep, 1)
                        dve.wait_ge(mxstep, 4 * sidx + k)
                    m, less = nm[:, 0, 0:n], nm[:, 1, 0:n]
                    step(nc.vector.tensor_reduce(m, nmt[:, a:a + n, :], X, ALU.min), 1)
                    step(nc.vector.tensor_copy(mp[:, 0:n, 0], m), 2)
                    step(nc.vector.tensor_tensor(less, m, mp[:, 0:n, 0], ALU.subtract), 3)
                    step(nc.vector.tensor_copy(mp[:, 0:n, 1], less), 4)
                    nc.vector.tensor_tensor(mp[:, 0:n, 2], less, mp[:, 0:n, 1], ALU.subtract).then_inc(negm, 1)

                def reciprocals(sidx, i):
                    if i == 0:
                        dve.wait_ge(d_ready, sidx + 2)
                        dve.wait_ge(fin_done, sidx + 1)
                    ins = nc.vector.reciprocal(Rr[:, i * QUART:(i + 1) * QUART], PS[:, 7, i * QUART:(i + 1) * QUART])
                    if i == 3:
                        ins.then_inc(recip, 1)

                def front_at(j):
                    if j == 0:
                        front_stats(g + 1)
                    elif j == 3:
                        squares(g + 1, 0, front)
                    elif j == 4:
                        var_eps(g + 1, 0, front)
                    elif j == 6:
                        front_bias(g + 1)
                    elif j == 8:
                        front_mid(g + 1)
                    elif j == 15:
                        front_sum_squares(g + 1)
                    elif j == 18:
                        front_parts(g + 1)
                    elif j == 19:
                        front_centre(g + 1)
                    elif j == 22:
                        front_channel_filter(g + 1)

                def superblock(sidx, half, base, first):
                    if half == 2:
                        assert n[0] == LINKS, n[0]
                    for j in range(NQ):
                        if half == 2 and more:
                            front_at(j)
                        if half < 2:
                            for i in tiles_at(NQ * half + j):
                                max_tile(i, base, PLAN[i][1])
                            if j == SPLIT_STEP:
                                dve.wait_ge(mx_free, base + (3 * TILES if half == 0 else PAIR_TILES) + 1)
                                if half == 0:
                                    split_max(sidx + 1, 0, 6)
                                else:
                                    split_max(sidx + 1, 6, 8)
                        if FINISH_STEP <= j < FINISH_STEP + 4 and not first:
                            reciprocals(sidx - 1, j - FINISH_STEP)
                        if j in DVE_SUMS:
                            r = key_rows(j)
                            dve.wait_ge(exp_done, NQ * sidx + j + 1)
                            e = Pb[0:r, j % PSLOTS, :, :]
                            if j == DVE_SUMS[0]:
                                dve.wait_ge(d_ready, sidx + 1)
                                nc.vector.tensor_copy(accD[0:r, :, :], e).then_inc(psum_dve, 1)
                            else:
                                dve.wait_ge(psum_dve, NDVE * (sidx + 1) + dve_sums_upto(j) - 1)
                                nc.vector.tensor_tensor(accD[0:r, :, :], accD[0:r, :, :], e,
                                                        ALU.add).then_inc(psum_dve, 1)

                for i in range(FIRST_TILES):
                    first_tile(i)
                dve.wait_ge(first_used, FIRST_TILES * (g + 1) + NJ)
                split_max(NJ * g, 0, 8)

                def pair_of(t, first):
                    base = GROUP_TILES * g + PAIR_TILES * t
                    superblock(NJ * g + 2 * t, 0, base, first)
                    superblock(NJ * g + 2 * t + 1, 1, base, False)

                pair_of(0, True)
                with dve.Fori(1, NJ // 2) as t:
                    pair_of(t, False)
                superblock(NJ * g + NJ - 1, 2, 0, False)
                for i in range(4):
                    reciprocals(NJ * g + NJ - 1, i)

            front_stats(0)
            centre_weights()
            squares(0, 0, front)
            var_eps(0, 0, front)
            front_bias(0)
            front_mid(0)
            tap_constants()
            front_sum_squares(0)
            front_parts(0)
            front_centre(0)
            front_channel_filter(0)
            with dve.Fori(0, GROUPS - 1) as g:
                group(g, True)
            group(GROUPS - 1, False)

        @block.scalar
        def _(act):
            act.sem_inc(pv_done, PSLOTS)
            act.wait_ge(borders, 1)
            act.wait_ge(setup, 1)
            act.wait_ge(cleared, 5)
            def normalise_chunk(dst, src, j, done):
                nc.scalar.activation(dst, rows(src[:, j * CH:(j + 1) * CH]), ACT.Identity,
                                     bias=nb[:, :], scale=rstd[:, :]).then_inc(done, 1)

            def padded(t, j):
                return pad_rows(t, ROWS * j + 1, ROWS, 1)

            def load_table(func):
                nc.scalar.activation(junk[:, 0:1], ones[:, 0:1], func)

            def front_normalise(g, j):
                if j == 0:
                    act.wait_ge(gn_nb[0], g + 1)
                normalise_chunk(padded(xnp, j), xin, j, xn_ready[0])

            def front_root(g):
                act.wait_ge(sfvar_ready, g + 1)
                nc.scalar.activation(sfs[:, 4, :], sfs[:, 2, :], ACT.Sqrt,
                                     scale=1.0 / (TAPS - 1)).then_inc(sfsd_ready, 1)

            def front_spatial_filter(g, j):
                act.wait_ge(sft_ready, NJ * g + j + 1)
                nc.scalar.activation(rows(SF[:, j * CH:(j + 1) * CH]), pad_rows(sTb[0:3 * PITCH, j % 2, :], 0, ROWS),
                                     ACT.Copy).then_inc(SF_ready, 1)

            def group(g, more):
                load_table(ACT.Sigmoid)
                act.wait_ge(gn_nb[1], g + 1)
                for j in range(4):
                    normalise_chunk(padded(xnp, j), xw, j, xn_ready[1])
                act.wait_ge(U_ready, g + 1)
                for j in range(NJ):
                    if j + 3 < NJ and j:
                        normalise_chunk(padded(xnp, j + 3), xw, j + 3, xn_ready[1])
                    act.wait_ge(l1_ps, NJ * g + j + 1)
                    if j >= 2:
                        act.wait_ge(gated_ready, NJ * g + j - 1)
                    nc.scalar.activation(att[:, j % 2, :], PS[:, 3 + j % 3, 0:CH], ACT.Sigmoid,
                                         bias=uc[:, 1:2]).then_inc(att_ready, 1)
                act.wait_ge(gn_nb[2], g + 1)
                normalise_chunk(padded(xh, 0), xw, 0, xh_ready)
                normalise_chunk(padded(xh, 1), xw, 1, xh_ready)
                normalise_chunk(padded(xnp, 0), xw, 0, xn_ready[2])
                normalise_chunk(padded(xnp, 1), xw, 1, xn_ready[2])
                for j in range(2, NJ):
                    normalise_chunk(padded(xh, j), xw, j, xh_ready)
                    normalise_chunk(padded(xnp, j), xw, j, xn_ready[2])
                act.wait_ge(gn_nb[3], g + 1)
                for j in range(NJ):
                    normalise_chunk(rows(xnf[:, j * CH:(j + 1) * CH]), xw, j, xn_ready[3])

                def middle_part(j):
                    act.wait_ge(rest_h, NJ * g + j + 1)
                    nc.scalar.activation(parts[:, 1, j * CH:(j + 1) * CH], rest[:, j, :],
                                         ACT.Copy).then_inc(part_m, 1)

                for j in range(NJ):
                    act.wait_ge(qk_ps, NJ * g + j + 1)
                    if j == 0:
                        for loaded in qk_loaded:
                            act.wait_ge(loaded, 16 * (SPREADS * g + 1))
                    nc.scalar.activation(parts[:, 0, j * CH:(j + 1) * CH], PS[0:4 * DK, j, 0:CH],
                                         ACT.Copy).then_inc(part_h, 1)
                for j in range(NJ):
                    middle_part(j)
                for i in range(NJ):
                    m = min(4, NQ - 4 * i)
                    r = key_rows(NQ - 1) if m < 4 else QC
                    act.wait_ge(v_ps, NJ * g + i + 1)
                    nc.scalar.activation(VT[0:r, 4 * i:4 * i + m, :],
                                         PS[0:r, i, 0:m * P].rearrange("p (a b) -> p a b", b=P),
                                         ACT.Copy).then_inc(v_ready, 1)

                def max_rows(sidx, col, n):
                    act.wait_ge(mrow_ps, sidx + 1)
                    nc.scalar.activation(Qa[KROWS:KROWS + 3, :, ds(col, n * BLK)],
                                         rowb[KROWS:KROWS + 3, :].rearrange("p (h n) -> p h n", h=2)[:, :, 0:n * BLK],
                                         ACT.Copy).then_inc(mrow, 1)

                def exps(sidx, steps, odd, rows_of=None, front_of=None):
                    for j in steps:
                        r = key_rows(j)
                        act.wait_ge(st_ready, NQ * sidx + j + 1)
                        act.wait_ge(pv_done, NQ * sidx + j + 1)
                        i = (j - PSLOTS) % NQ
                        if i in DVE_SUMS:
                            act.wait_ge(psum_dve, NDVE * (sidx + (j >= PSLOTS)) + dve_sums_upto(i))
                        else:
                            act.wait_ge(psum_pool, POOL_SUMS * (sidx + (j >= PSLOTS)) + pool_sums_upto(i))
                        b = 2 * ((j + odd) % 2)
                        nc.scalar.activation(Pb[0:r, j % PSLOTS, :, :], PS[0:r, b:b + 2, 0:CH],
                                             ACT.Exp).then_inc(exp_done, 1)
                        if j == ROWS_STEP + 2 and rows_of:
                            max_rows(sidx + 1, *rows_of)
                        if front_of is not None:
                            if FRONT_XN <= j < FRONT_XN + NJ:
                                front_normalise(front_of, j - FRONT_XN)
                            for i in range(NJ):
                                if FRONT_TR[i] == j - 1:
                                    front_spatial_filter(front_of, i)
                            if j == FRONT_ROOT:
                                front_root(front_of)

                def copy_output(sidx):
                    act.wait_ge(pv_done, NQ * (sidx + 1) + PSLOTS)
                    act.wait_ge(fin_done, sidx + 1)
                    nc.scalar.activation(Osb[:, :], PS[:, OB, 0:CH], ACT.Copy).then_inc(ocopy, 1)

                load_table(ACT.Exp)
                max_rows(NJ * g, 0, 4)
                exps(NJ * g, range(0, TURN), 0)
                with act.Fori(0, NJ // 2) as t:
                    n = NJ * g + 2 * t
                    exps(n, range(TURN, NQ), 0, (2 * CH * t + 4 * BLK, 3))
                    exps(n + 1, range(0, 1), 1)
                    copy_output(n)
                    exps(n + 1, range(1, NQ), 1, (2 * CH * t + 2 * CH, 4))
                    exps(n + 2, range(0, 1), 0)
                    copy_output(n + 1)
                    exps(n + 2, range(1, TURN), 0)
                exps(NJ * g + NJ - 1, range(TURN, NQ), 0, None, g + 1 if more else None)
                if more:
                    for j in range(NJ):
                        if FRONT_TR[j] == NQ - 1:
                            front_spatial_filter(g + 1, j)
                copy_output(NJ * g + NJ - 1)

            for j in range(NJ):
                front_normalise(0, j)
            front_root(0)
            for j in range(NJ):
                front_spatial_filter(0, j)
            with act.Fori(0, GROUPS - 1) as g:
                group(g, True)
            group(GROUPS - 1, False)

        @block.gpsimd
        def _(pool):
            pool.sem_inc(psum_pool, POOL_SUMS)
            pool.sem_inc(pooltaps, 1)
            pool.sem_inc(pool_step, POOL_STEPS)
            for i, (t, value) in enumerate(((xh[:, :].bitcast(F32), 0.0), (xl[:, :].bitcast(F32), 0.0),
                                            (Qa[:, :, HW:HWQ], 0.0), (VT[key_rows(NQ - 1):QC, NQ - 1, :], 0.0),
                                            (Ka[KROWS:KROWS + 3, :, :], 1.0))):
                nc.gpsimd.memset(t, value).then_inc(cleared, 1)
                pool.wait_ge(cleared, i + 1)
            pool.wait_ge(setup, 1)

            def power(g, layer):
                pool.wait_ge(gn_ve[layer], g + 1)
                nc.gpsimd.tensor_tensor(rstd[:, :], ve[:, :], mhalf[:, :], ALU.pow).then_inc(gn_rstd[layer], 1)

            def channel_root(g):
                pool.wait_ge(yvar_ready, g + 1)
                nc.gpsimd.tensor_tensor(ys[:, 4:5], ys[:, 3:4], phalf[:, :], ALU.pow).then_inc(ysd_ready, 1)

            def group(g, more):
                with pool.Fori(0, NJ) as j:
                    k = NJ * g + j
                    pool.wait_ge(pooltaps, k + 1)
                    pool.wait_ge(prod_ready, TAPS * k + 4 + TAP_BANKS)
                    nc.gpsimd.tensor_tensor(pu[:, 0, :], prod[:, 1, :], prod[:, 3, :], ALU.add).then_inc(pool_step, 1)
                    pool.wait_ge(pool_step, POOL_STEPS * (k + 1) + 1)
                    nc.gpsimd.tensor_tensor(pu[:, 1, :], pu[:, 0, :], xin[:, ds(j * CH, CH)], ALU.add).then_inc(pool_step, 1)
                    pool.wait_ge(pool_step, POOL_STEPS * (k + 1) + 2)
                    pool.wait_ge(prod_ready, TAPS * k + 6 + TAP_BANKS)
                    nc.gpsimd.tensor_tensor(pu[:, 0, :], pu[:, 1, :], prod[:, 5, :], ALU.add).then_inc(pool_step, 1)
                    pool.wait_ge(pool_step, POOL_STEPS * (k + 1) + 3)
                    pool.wait_ge(prod_ready, TAPS * k + 8 + TAP_BANKS)
                    pool.wait_ge(l0_done, k + 2)
                    nc.gpsimd.tensor_tensor(pu[:, 2, :], pu[:, 0, :], prod[:, 7, :], ALU.add).then_inc(pooltaps, 1)
                power(g, 1)
                for j in range(NJ):
                    c = slice(j * CH, (j + 1) * CH)
                    pool.wait_ge(gated_ready, NJ * g + j + 1)
                    nc.gpsimd.tensor_tensor(xw[:, c], xw[:, c], gated[:, j % 2, :], ALU.add).then_inc(l1_done, 1)
                power(g, 2)
                power(g, 3)

                def finish(sidx, s):
                    pool.wait_ge(ocopy, sidx + 2)
                    pool.wait_ge(recip, sidx + 2)
                    nc.gpsimd.tensor_tensor(fin[:, :], Osb[:, :], Rr[:, :], ALU.mult).then_inc(fin_step, 1)
                    pool.wait_ge(fin_step, sidx + 1)
                    nc.gpsimd.tensor_tensor(xw[:, ds(s * CH, CH)], xw[:, ds(s * CH, CH)], fin[:, :],
                                            ALU.add).then_inc(fin_done, 1)

                def superblock(sidx, s, first, front=False):
                    for j in range(1, NQ):
                        if front and j == 5:
                            power(g + 1, 0)
                        if front and j == 21:
                            channel_root(g + 1)
                        if j not in DVE_SUMS:
                            pool.wait_ge(exp_done, NQ * sidx + j + 1)
                            if j == 1:
                                nc.gpsimd.tensor_tensor(accQ[:, :, :], Pb[:, 0, :, :], Pb[:, 1, :, :],
                                                        ALU.add).then_inc(psum_pool, 2)
                                continue
                            if j == TO_ACCP:
                                pool.wait_ge(d_ready, sidx + 1)
                            pool.wait_ge(psum_pool, POOL_SUMS * (sidx + 1) + pool_sums_upto(j) - 1)
                            nc.gpsimd.tensor_tensor((accQ if j < TO_ACCP else accP)[:, :, :],
                                                    (accQ if j <= TO_ACCP else accP)[:, :, :],
                                                    Pb[:, j % PSLOTS, :, :], ALU.add).then_inc(psum_pool, 1)
                        if j == FINISH_STEP + 5 and not first:
                            finish(sidx - 1, s - 1)

                superblock(NJ * g, 0, True)
                with pool.Fori(1, NJ - 1) as s:
                    superblock(NJ * g + s, s, False)
                superblock(NJ * g + NJ - 1, NJ - 1, False, more)
                finish(NJ * g + NJ - 1, NJ - 1)

            power(0, 0)
            channel_root(0)
            with pool.Fori(0, GROUPS - 1) as g:
                group(g, True)
            group(GROUPS - 1, False)

        @block.tensor
        def _(pe):
            mm = nc.tensor.matmul
            pe.sem_inc(tap_added, PE_TAPS)
            pe.sem_inc(l0_done, 2)
            pe.wait_ge(w_loaded, 3 * 16)
            pe.wait_ge(consts, 2)
            pe.wait_ge(setup, 1)
            pe.wait_ge(cleared, 5)

            def pair_mean(g, layer, bank):
                pe.wait_ge(gn_mean[layer], g + 1)
                mm(bank[:, 0:1], pair, mv[:, 0:1], start=True, stop=True).then_inc(gn_pm[layer], 1)

            def pair_var(g, layer, bank):
                pe.wait_ge(gn_sq[layer], g + 1)
                mm(bank[:, 1:2], pair, sq[:, :], start=True, stop=True).then_inc(gn_pv[layer], 1)

            def front_mid(g):
                pe.wait_ge(pooled_ready, 2 * g + 1)
                mm(front[0:2 * MID, 2:3], wcol("w1"), pooled[:, 0:1], start=True, stop=True).then_inc(mid_ready, 1)

            def front_channel_filter(g):
                pe.wait_ge(y1_ready, g + 1)
                for t in range(TAPS):
                    last = mm(small[:, 8 + t:9 + t], wcol("w2")[0:2 * MID, t * P:(t + 1) * P], y1[:, :],
                              start=True, stop=True)
                last.then_inc(y_ready, 1)

            def front_spatial_filter(g, j):
                pe.wait_ge(xn_ready[0], NJ * g + j + 1)
                for i in range(4 * j, 4 * j + 4):
                    last = mm(PS[0:SP2, SFB, i * PART:(i + 1) * PART], xnp[:, (2 * i + 1) * PW + 1:(2 * i + 3) * PW + 1],
                              wcol("ws"), start=True, stop=True)
                if j == NJ - 1:
                    last.then_inc(sfT_ready, 1)

            def front_transpose(g, j):
                if j == 0:
                    pe.wait_ge(sfp_ready, g + 1)
                if j >= 2:
                    pe.wait_ge(SF_ready, NJ * g + j - 1)
                for i in range(4):
                    last = nc.tensor.transpose(sTb[0:3 * PITCH, j % 2, i * SP2:(i + 1) * SP2],
                                               sfp[:, 4 * j + i, :, :].rearrange("p a b -> p (a b)"),
                                               identb[0:SP2, 0:SP2])
                last.then_inc(sft_ready, 1)

            def group(g, more):
                def pair_stats(layer):
                    pair_mean(g, layer, small)
                    pair_var(g, layer, small)

                def spread_tap(j, t):
                    k = NJ * g + j
                    pe.wait_ge(prod_ready, TAPS * k + t + 1)
                    mm(PS[:, t % TAP_BANKS, 0:CH], selb[:, t, :], SF[:, ds(j * CH, CH)],
                       start=True, stop=True).then_inc(tap_ready, 1)

                def add_tap(j, odd, t):
                    k = NJ * g + j
                    pe.wait_ge(prod_ready, TAPS * k + t + 1 + TAP_BANKS)
                    if t == 0:
                        pe.wait_ge(l0_done, k + 1)
                    mm(PS[:, ACCB + odd, 0:CH], identf, prod[:, t, :], start=(t == 0),
                       stop=(t == TAPS - 1)).then_inc(tap_added, 1)

                def taps(j, odd, first):
                    for t in range(TAPS):
                        spread_tap(j, t)
                        if t in (1, 2) and not first:
                            add_tap(j - 1, 1 - odd, 4 + 2 * t)
                        if t in (3, 5, 7):
                            add_tap(j, odd, t - 3)

                pe.wait_ge(SF_ready, NJ * (g + 1))
                taps(0, 0, True)
                with pe.Fori(0, NJ // 2) as i:
                    taps(2 * i + 1, 1, False)
                    taps(2 * i + 2, 0, False)
                add_tap(NJ - 1, 0, TAPS - 3)
                add_tap(NJ - 1, 0, TAPS - 1)

                pair_stats(1)
                pe.wait_ge(pooled_ready, 2 * g + 2)
                mm(small[0:2 * CR, 20:21], wcol("wk"), pooled[:, 1:2], start=True, stop=True).then_inc(km_ps, 1)
                pe.wait_ge(km_ready, g + 1)
                mm(small[:, 21:22], wcol("wq")[0:2 * CR], km[:, 0:1], start=True, stop=True)
                mm(small[:, 22:23], half8[0:2 * CR], km[:, 1:2], start=True, stop=True).then_inc(u_ps, 1)
                for j in range(NJ):
                    pe.wait_ge(xn_ready[1], NJ * g + j + 1)
                    if j == 0:
                        pe.wait_ge(U_ready, g + 1)
                    if j >= 3:
                        pe.wait_ge(gated_ready, NJ * g + j - 2)
                    xnj = pad_rows(xnp, ROWS * j + 1, ROWS, 1)
                    mm(PS[:, j % 3, 0:CH], wcol("wv"), xnj, start=True, stop=True)
                    mm(PS[:, 3 + j % 3, 0:CH], U[:, :], xnj, start=True, stop=True).then_inc(l1_ps, 1)

                pair_stats(2)
                def convolve(j, need):
                    for src, ready in ((xh, xh_ready), (xl, xl_ready)):
                        pe.wait_ge(ready, NJ * g + need)
                        for t in range(TAPS):
                            last = mm(PS[:, j, 0:CH], wt[:, t * P:(t + 1) * P],
                                      pad_rows_at(src, j * (ROWS * PW) + (t // 3) * PW + t % 3, ROWS),
                                      start=(src is xh and t == 0), stop=(src is xl and t == TAPS - 1))
                    last.then_inc(conv_ready, 1)

                with pe.Fori(0, NJ - 1) as j:
                    convolve(j, j + 2)
                convolve(NJ - 1, NJ)

                pair_stats(3)
                for j in range(NJ):
                    pe.wait_ge(xn_ready[3], NJ * g + j + 1)
                    mm(PS[0:4 * DK, j, 0:CH], wcol("qk3"), xnf[:, j * CH:(j + 1) * CH],
                       start=True, stop=True).then_inc(qk_ps, 1)
                for j in range(NQ):
                    r = key_rows(j)
                    if j % 4 == 0:
                        pe.wait_ge(rest_h, NJ * g + j // 4 + 1)
                    last = mm(PS[0:r, j // 4, (j % 4) * P:(j % 4 + 1) * P], xnf[:, j * QC:j * QC + r], wcol("wv3"),
                              start=True, stop=True)
                    if j % 4 == 3 or j == NQ - 1:
                        last.then_inc(v_ps, 1)

                def max_tile(i, base, bank, left, col):
                    blk, h, t = i // TILES, i // NJ % 2, i % NJ
                    pe.wait_ge(mx_free, base + left + 1)
                    mm(PS[0:BLK, bank, 0:CH], Qa[0:KROWS, h, ds(col + blk * BLK, BLK)],
                       Ka[0:KROWS, h, t * CH:(t + 1) * CH], start=True, stop=True).then_inc(mx_ready, 1)

                def max_rows(sidx, n):
                    pe.wait_ge(negm, sidx + 1)
                    for i in range(2 * n):
                        at = (i % 2) * 4 * BLK + (i // 2) * BLK
                        last = nc.tensor.transpose(rowb[KROWS:KROWS + 3, at:at + BLK], mp[:, i, :], identb[:, :])
                    last.then_inc(mrow_ps, 1)

                def scores(k, s, h):
                    j = k % NQ
                    r = key_rows(j)
                    ins = mm(PS[0:r, 2 * (k % 2) + h, 0:CH], Ka[0:KROWS + 3, h, j * QC:j * QC + r],
                             Qa[0:KROWS + 3, h, ds(s * CH, CH)], start=True, stop=True)
                    if h == 1:
                        ins.then_inc(st_ready, 1)

                def denominators(sidx):
                    pe.wait_ge(psum_pool, POOL_SUMS * (sidx + 2))
                    pe.wait_ge(psum_dve, NDVE * (sidx + 2))
                    for h in range(2):
                        mm(PS[C * h:C * h + C, 7, 0:CH], ones[:, :], accP[:, h, :], start=True, stop=False)
                        last = mm(PS[C * h:C * h + C, 7, 0:CH], ones[:, :], accD[:, h, :], start=False, stop=True)
                    last.then_inc(d_ready, 1)

                def front_at(j):
                    if j == 2:
                        pair_mean(g + 1, 0, front)
                    elif j == 3:
                        pair_var(g + 1, 0, front)
                    elif j == 7:
                        front_mid(g + 1)
                    elif j == 16:
                        pe.wait_ge(recip, NJ * g + NJ)
                        front_channel_filter(g + 1)
                    if FRONT_SF <= j < FRONT_SF + NJ:
                        front_spatial_filter(g + 1, j - FRONT_SF)
                    for i in range(NJ):
                        if FRONT_TR[i] == j:
                            front_transpose(g + 1, i)

                def superblock(s, half, base, col, first):
                    sidx = NJ * g + s
                    seen7 = False
                    for j in range(NQ):
                        k = NQ * (half % 2) + j
                        tiles = [] if half == 2 else [i for i in tiles_at(k) if not first or i >= EARLY_TILES]

                        def next_tile(seen7):
                            if tiles:
                                i = tiles.pop(0)
                                if PLAN[i][1] == 7 and not seen7:
                                    pe.wait_ge(recip, sidx + 1)
                                    seen7 = True
                                max_tile(i, base, PLAN[i][1], PLAN[i][2], col)
                            return seen7
                        pe.wait_ge(exp_done, NQ * sidx + j + 1)
                        if j == 0:
                            pe.wait_ge(ocopy, sidx + 1)
                        for h in range(2):
                            last = mm(PS[C * h:C * h + C, OB, 0:CH], VT[:, j, C * h:C * h + C],
                                      Pb[:, j % PSLOTS, h, :], start=(j == 0), stop=(j == NQ - 1))
                        last.then_inc(pv_done, 1)
                        for h in range(2):
                            if j < NQ - 2 or half < 2:
                                if j == NQ - 2 and h == 0:
                                    pe.wait_ge(mrow, sidx + 2)
                                scores(k + 2, s + (j >= NQ - 2), h)
                            seen7 = next_tile(seen7)
                        while tiles:
                            seen7 = next_tile(seen7)
                        if j == FINISH_STEP - 1 and not first:
                            denominators(sidx - 1)
                        if half == 2 and more:
                            front_at(j)
                        if j == ROWS_STEP and half < 2:
                            max_rows(sidx + 1, 3 + half)

                def pair_of(t, first):
                    base = GROUP_TILES * g + PAIR_TILES * t
                    col = 2 * CH * t + 4 * BLK
                    superblock(2 * t, 0, base, col, first)
                    superblock(2 * t + 1, 1, base, col, False)

                pe.wait_ge(v_ready, NJ * (g + 1))
                for i in range(FIRST_TILES):
                    h, blk, t = i // (FIRST_TILES // 2), i // NJ % 4, i % NJ
                    if i % (FIRST_TILES // 2) == 0:
                        pe.wait_ge(qk_loaded[h], 16 * (SPREADS * (g + 1) + 1))
                    pe.wait_ge(first_used, FIRST_TILES * g + i + 1)
                    mm(PS[0:BLK, t, 0:CH], Qa[0:KROWS, h, blk * BLK:(blk + 1) * BLK],
                       Ka[0:KROWS, h, t * CH:(t + 1) * CH], start=True, stop=True).then_inc(first_ready, 1)
                max_rows(NJ * g, 4)
                for i in range(EARLY_TILES):
                    max_tile(i, GROUP_TILES * g, PLAN[i][1], 0, 4 * BLK)
                pe.wait_ge(mrow, NJ * g + 1)
                for j in range(2):
                    for h in range(2):
                        scores(j, 0, h)
                pair_of(0, True)
                with pe.Fori(1, NJ // 2) as t:
                    pair_of(t, False)
                superblock(NJ - 1, 2, 0, 0, False)
                denominators(NJ * g + NJ - 1)

            pair_mean(0, 0, front)
            pair_var(0, 0, front)
            front_mid(0)
            for j in range(NJ):
                front_spatial_filter(0, j)
            front_channel_filter(0)
            pe.wait_ge(ternary, 2)
            for j in range(NJ):
                front_transpose(0, j)
            with pe.Fori(0, GROUPS - 1) as g:
                group(g, True)
            group(GROUPS - 1, False)


def constants(np):
    c = np.zeros((P, CCOLS), np.float32)
    p = np.arange(P)
    c[:, 0:P] = np.eye(P)
    c[:, P:2 * P] = 0.5 * (p[:, None] // 2 == p[None, :] // 2)
    c[:, 2 * P:3 * P] = p[:, None] // C == p[None, :] // C
    c[0:2 * CR, 3 * P:4 * P] = p[0:2 * CR, None] // CR == p[None, :] // C
    for part in range(3):
        for h in range(2):
            for t in range(TAPS):
                a = 4 * P + t * P + C * h
                c[part * PITCH + h * TAPS + t, a:a + C] = 1.0
    return c


def kernel(**inputs):
    import numpy as np
    import concourse.bacc as bacc
    from concourse.bass_utils import run_bass_kernel_spmd

    a = {k: np.asarray(w) for k, w in inputs.items()}
    arrays = {"x": a["x"].reshape(GROUPS, P, HW), "weights": np.zeros((P, WCOLS), np.float32),
              "vectors": np.zeros((P, VCOLS), np.float32), "cst": constants(np)}

    def put(name, block, at, row):
        col = COLS[name][0] + at
        arrays["weights"][row:row + block.shape[0], col:col + block.shape[1]] = block

    def put_vector(name, row, block):
        arrays["vectors"][row:row + block.shape[0], VEC[name][0]:VEC[name][1]] = block

    w2 = a["L0_conv_w2"].reshape(C, TAPS, MID)
    wc = a["L2_conv_weight"].reshape(C, C, TAPS)
    for h in range(2):
        put("w1", a["L0_conv_w1"].T, MID * h, C * h)
        put("ws", a["L0_conv_ws"].T, TAPS * h, C * h)
        put("wv", a["L1_conv_Wv"].T, C * h, C * h)
        put("wk", a["L1_conv_Wk"].T, CR * h, C * h)
        put("wq", a["L1_conv_Wq"], C * h, CR * h)
        put("qk3", a["L3_conv_q_w"].T, 2 * DK * h, C * h)
        put("qk3", a["L3_conv_k_w"].T, 2 * DK * h + DK, C * h)
        put("wv3", a["L3_conv_v_w"].T, C * h, C * h)
        for t in range(TAPS):
            put("w2", w2[:, t].T, t * P + C * h, MID * h)
            put("conv", wc[:, :, t].T, t * P + C * h, C * h)
        put_vector("b2", C * h, a["L0_conv_b2"].reshape(C, TAPS))
        put_vector("fn", C * h, a["L0_conv_fn_std"].reshape(C, TAPS))
        put_vector("bs", C * h, np.broadcast_to(a["L0_conv_bs"], (C, TAPS)))
        put_vector("b1", MID * h, a["L0_conv_b1"].reshape(MID, 1))
        put_vector("bk", CR * h, a["L1_conv_bk"].reshape(CR, 1))
        put_vector("bq", CR * h, a["L1_conv_bq"].reshape(CR, 1))
        put_vector("bv", C * h, a["L1_conv_bv"].reshape(C, 1))
        put_vector("bc", C * h, a["L2_conv_bias"].reshape(C, 1))
    nc = bacc.Bacc("TRN2", target_bir_lowering=False, num_devices=1)
    arrays = {f"in_{k}": np.ascontiguousarray(w) for k, w in arrays.items()}
    args = [nc.dram_tensor(k, w.shape, mybir.dt.from_np(w.dtype), kind="ExternalInput").ap()
            for k, w in arrays.items()]
    out = nc.dram_tensor("out", (GROUPS, P, HW), F32, kind="ExternalOutput").ap()
    build(nc, *args, out)
    r = run_bass_kernel_spmd(nc, [arrays], core_ids=[0])
    return r.results[0]["out"].reshape(B, C, H, W)
```
